# Optimizing a Trainium2 kernel written in Bass

```python
import numpy as np
import jax
import jax.numpy as jnp

def _softmax(x, axis=-1):
    return jax.nn.softmax(x, axis=axis)

def _gelu(x):
    return jax.nn.gelu(x, approximate=True)

def _silu(x):
    return jax.nn.silu(x)

def _sigmoid(x):
    return jax.nn.sigmoid(x)

def _layernorm(x, axis=-1, eps=1e-05):
    m = jnp.mean(x, axis=axis, keepdims=True)
    v = jnp.var(x, axis=axis, keepdims=True)
    return (x - m) / jnp.sqrt(v + eps)

def _scatter_add(tgt, idx, src, axis=0):
    return tgt.at[idx].add(src)

def _segment_sum(src, seg, n):
    return jax.ops.segment_sum(src, seg, n)
kernel_name = 'mk_decoder_preln_d1_seqx_r8_87e9a8'

def setup_inputs(seed: int=0):
    np.random.seed(seed)
    _w = jnp.asarray

    def _rec_inputs():
        import jax
        import jax.numpy as jnp
        _rk = jax.random.key(seed)
        x = -0.000125 + 0.9999 * jax.random.normal(jax.random.fold_in(_rk, 1), (8, 128, 512), jnp.float32)
        _lenS = 128 - jax.random.randint(jax.random.fold_in(_rk, 7), (8,), 0, max(1, 128 // 4) + 1, jnp.int32)
        _lenS2 = 128 - jax.random.randint(jax.random.fold_in(_rk, 8), (8,), 0, max(1, 128 // 4) + 1, jnp.int32)
        _ctx_4096P = jax.random.normal(jax.random.fold_in(_rk, 11), (8, 16, 512), jnp.float32)
        _ctx_4096c = jax.random.dirichlet(jax.random.fold_in(_rk, 511), 0.3 * jnp.ones((16,), jnp.float32), (8, 128))
        _ctx_4096t = jnp.einsum('bsk,bkd->bsd', _ctx_4096c, _ctx_4096P)
        _ctx_4096t = _ctx_4096t * jax.lax.rsqrt(jnp.mean(jnp.square(_ctx_4096t)) + 1e-12) * 0.953939
        ctx_4096 = -1.52775e-05 + 0.999936 * (_ctx_4096t + 0.3 * jax.random.normal(jax.random.fold_in(_rk, 611), (8, 128, 512), jnp.float32))
        return (x, ctx_4096)
    x, ctx_4096 = _rec_inputs()

    def _L0_attn_setup():
        import math
        import jax, jax.numpy as jnp
        import numpy as np
        NUM_HEADS = 32
        HIDDEN = 512
        HEAD_DIM = HIDDEN // NUM_HEADS
        NEG_INF = -1e+30

        def _alibi_slopes(n: int) -> jnp.ndarray:
            cp2 = 2 ** math.floor(math.log2(n))
            base = 2.0 ** (-2.0 ** (-(math.log2(cp2) - 3)))
            slopes = base ** np.arange(1, cp2 + 1, dtype=np.float64)
            if cp2 != n:
                extra_base = 2.0 ** (-2.0 ** (-(math.log2(2 * cp2) - 3)))
                rem = min(cp2, n - cp2)
                extra = extra_base ** np.arange(1, 1 + 2 * rem, 2, dtype=np.float64)
                slopes = np.concatenate([slopes, extra])
            return jnp.asarray(slopes, dtype=jnp.float32)
        key = jax.random.key(seed)
        k1, k2, k3 = jax.random.split(key, 3)
        B, S = (2, 256)
        hidden_states = jax.random.normal(k1, (B, S, HIDDEN), dtype=jnp.float32)
        Wqkv = jax.random.normal(k2, (HIDDEN, NUM_HEADS * HEAD_DIM + 2 * HEAD_DIM), dtype=jnp.float32) * 0.02
        Wo = jax.random.normal(k3, (HIDDEN, HIDDEN), dtype=jnp.float32) * 0.02
        return {'hidden_states': hidden_states, 'Wqkv': Wqkv, 'Wo': Wo}
    _L0_attn_all = _L0_attn_setup()
    _L0_attn_in = {k: v for k, v in _L0_attn_all.items() if k in ('Wqkv', 'Wo')}
    del _L0_attn_all

    def _L0_xattn_setup():
        import jax, jax.numpy as jnp
        import numpy as np
        H = 8
        C = 2

        def _autocorrelation(Q, K, V):
            B, L, D = Q.shape
            d = D // H
            q = Q.reshape(B, L, H, d).transpose(0, 2, 1, 3)
            k = K.reshape(B, L, H, d).transpose(0, 2, 1, 3)
            v = V.reshape(B, L, H, d).transpose(0, 2, 1, 3)
            qf = jnp.fft.fft(q, axis=2)
            kf = jnp.fft.fft(k, axis=2)
            corr = jnp.fft.ifft(qf * jnp.conj(kf), axis=2).real
            topk = int(C * np.log(L))
            w, idx = jax.lax.top_k(corr.transpose(0, 1, 3, 2), topk)
            w = jax.nn.softmax(w, axis=-1)
            pos = jnp.arange(L)[:, None]
            out = jnp.zeros_like(v)
            for i in range(topk):
                g = jnp.minimum(idx[:, :, None, :, i] + pos, L - 1)
                out = out + w[:, :, None, :, i] * jnp.take_along_axis(v, g, axis=2)
            return out.transpose(0, 2, 1, 3).reshape(B, L, D)
        key = jax.random.key(seed)
        k1, k2, k3 = jax.random.split(key, 3)
        B, L, D = (16, 64, 512)
        Q = jax.random.normal(k1, (B, L, D), dtype=jnp.float32)
        K = jax.random.normal(k2, (B, L, D), dtype=jnp.float32)
        V = jax.random.normal(k3, (B, L, D), dtype=jnp.float32)
        return {'Q': Q, 'K': K, 'V': V}
    _L0_xattn_all = _L0_xattn_setup()
    _L0_xattn_in = {k: v for k, v in _L0_xattn_all.items() if k in ()}
    del _L0_xattn_all

    def _L0_ffn_setup():
        import jax, jax.numpy as jnp
        import numpy as np
        IN_F = 512
        OUT_F = 512
        RANK = 8
        NUM_EXPERTS = 64
        TOP_K = 16
        ROUTER_DIM = 16
        ALPHA = 32
        SCALING = ALPHA / TOP_K
        BOTTLENECK = NUM_EXPERTS * RANK
        key = jax.random.key(seed)
        ks = jax.random.split(key, 5)
        x = jax.random.normal(ks[0], (4, 512, IN_F), dtype=jnp.float32)
        bound_a = float(np.sqrt(6.0 / IN_F))
        A_w = jax.random.uniform(ks[1], (BOTTLENECK, IN_F), jnp.float32, -bound_a, bound_a)
        B_w = jax.random.normal(ks[2], (OUT_F, BOTTLENECK), dtype=jnp.float32) * 0.02
        Wq_w = jax.random.normal(ks[3], (ROUTER_DIM, IN_F), dtype=jnp.float32) * 0.02
        keys = jax.random.normal(ks[4], (NUM_EXPERTS, ROUTER_DIM), dtype=jnp.float32) * 0.01
        return {'x': x, 'A_w': A_w, 'B_w': B_w, 'Wq_w': Wq_w, 'keys': keys}
    _L0_ffn_all = _L0_ffn_setup()
    _L0_ffn_in = {k: v for k, v in _L0_ffn_all.items() if k in ('A_w', 'B_w', 'Wq_w', 'keys')}
    del _L0_ffn_all
    return {'x': x, 'ctx_4096': ctx_4096, 'L0_attn_Wqkv': _L0_attn_in['Wqkv'], 'L0_attn_Wo': _L0_attn_in['Wo'], 'L0_ffn_A_w': _L0_ffn_in['A_w'], 'L0_ffn_B_w': _L0_ffn_in['B_w'], 'L0_ffn_Wq_w': _L0_ffn_in['Wq_w'], 'L0_ffn_keys': _L0_ffn_in['keys']}

def reference(x, ctx_4096, L0_attn_Wqkv, L0_attn_Wo, L0_ffn_A_w, L0_ffn_B_w, L0_ffn_Wq_w, L0_ffn_keys):
    import jax
    import jax.numpy as jnp

    def _L0_attn_ref(hidden_states, Wqkv, Wo):
        import math
        import jax, jax.numpy as jnp
        import numpy as np
        NUM_HEADS = 32
        HIDDEN = 512
        HEAD_DIM = HIDDEN // NUM_HEADS
        NEG_INF = -1e+30

        def _alibi_slopes(n: int) -> jnp.ndarray:
            cp2 = 2 ** math.floor(math.log2(n))
            base = 2.0 ** (-2.0 ** (-(math.log2(cp2) - 3)))
            slopes = base ** np.arange(1, cp2 + 1, dtype=np.float64)
            if cp2 != n:
                extra_base = 2.0 ** (-2.0 ** (-(math.log2(2 * cp2) - 3)))
                rem = min(cp2, n - cp2)
                extra = extra_base ** np.arange(1, 1 + 2 * rem, 2, dtype=np.float64)
                slopes = np.concatenate([slopes, extra])
            return jnp.asarray(slopes, dtype=jnp.float32)
        B, S, H = hidden_states.shape
        nH, d = (NUM_HEADS, HEAD_DIM)
        scale = d ** (-0.5)
        qkv = hidden_states @ Wqkv
        q = qkv[..., :nH * d].reshape(B, S, nH, d)
        k = qkv[..., nH * d:nH * d + d]
        v = qkv[..., nH * d + d:]
        scores = jnp.einsum('bqhd,bkd->bhqk', q, k) * scale
        pos_q = jnp.arange(S)[:, None]
        pos_k = jnp.arange(S)[None, :]
        slopes = _alibi_slopes(nH)
        alibi = slopes[:, None, None] * (pos_k - pos_q).astype(jnp.float32)
        causal = pos_k <= pos_q
        scores = jnp.where(causal[None, None], scores + alibi[None], NEG_INF)
        probs = jax.nn.softmax(scores, axis=-1)
        attn = jnp.einsum('bhqk,bkd->bqhd', probs, v).reshape(B, S, H)
        return attn @ Wo

    def _L0_xattn_ref(Q, K, V):
        import jax, jax.numpy as jnp
        import numpy as np
        H = 8
        C = 2

        def _autocorrelation(Q, K, V):
            B, L, D = Q.shape
            d = D // H
            q = Q.reshape(B, L, H, d).transpose(0, 2, 1, 3)
            k = K.reshape(B, L, H, d).transpose(0, 2, 1, 3)
            v = V.reshape(B, L, H, d).transpose(0, 2, 1, 3)
            qf = jnp.fft.fft(q, axis=2)
            kf = jnp.fft.fft(k, axis=2)
            corr = jnp.fft.ifft(qf * jnp.conj(kf), axis=2).real
            topk = int(C * np.log(L))
            w, idx = jax.lax.top_k(corr.transpose(0, 1, 3, 2), topk)
            w = jax.nn.softmax(w, axis=-1)
            pos = jnp.arange(L)[:, None]
            out = jnp.zeros_like(v)
            for i in range(topk):
                g = jnp.minimum(idx[:, :, None, :, i] + pos, L - 1)
                out = out + w[:, :, None, :, i] * jnp.take_along_axis(v, g, axis=2)
            return out.transpose(0, 2, 1, 3).reshape(B, L, D)
        return _autocorrelation(Q, K, V)

    def _L0_ffn_ref(x, A_w, B_w, Wq_w, keys):
        import jax, jax.numpy as jnp
        import numpy as np
        IN_F = 512
        OUT_F = 512
        RANK = 8
        NUM_EXPERTS = 64
        TOP_K = 16
        ROUTER_DIM = 16
        ALPHA = 32
        SCALING = ALPHA / TOP_K
        BOTTLENECK = NUM_EXPERTS * RANK
        q = jnp.einsum('bsd,rd->bsr', x, Wq_w)
        scores = jnp.einsum('bsr,er->bse', q, keys)
        top_vals, top_idx = jax.lax.top_k(scores, TOP_K)
        top_w = jax.nn.softmax(top_vals, axis=-1)
        gate = jnp.sum(jax.nn.one_hot(top_idx, NUM_EXPERTS, dtype=top_w.dtype) * top_w[..., None], axis=-2)
        z = jnp.einsum('bsd,nd->bsn', x, A_w)
        z = z.reshape(*z.shape[:-1], NUM_EXPERTS, RANK)
        z_gated = (z * gate[..., None]).reshape(*z.shape[:-2], BOTTLENECK)
        out = jnp.einsum('bsn,on->bso', z_gated, B_w) * SCALING
        return out
    x = x + _L0_attn_ref(_layernorm(x, axis=-1), L0_attn_Wqkv, L0_attn_Wo)
    x = x + _L0_xattn_ref(_layernorm(x, axis=-1), ctx_4096, ctx_4096)
    x = x + _L0_ffn_ref(_layernorm(x, axis=-1), L0_ffn_A_w, L0_ffn_B_w, L0_ffn_Wq_w, L0_ffn_keys)
    return x

_drawn_inputs = setup_inputs


def setup_inputs(seed=0):
    import zlib

    import numpy as np

    out = dict(_drawn_inputs(seed))
    spreads = {}
    factors = {}
    for name, (base, spread) in spreads.items():
        noise = np.random.default_rng([zlib.crc32(name.encode()), seed]).standard_normal(out[name].shape)
        drawn = base * np.exp(spread * noise) if base else spread * noise
        out[name] = jnp.asarray(drawn.astype(out[name].dtype))
    for name, factor in factors.items():
        out[name] = (out[name] * factor).astype(out[name].dtype)
    return out
```

```python
from contextlib import ExitStack

import concourse.bass as bass
from concourse import mybir

F32 = mybir.dt.float32
F32R = mybir.dt.float32r
BF16 = mybir.dt.bfloat16
ALU = mybir.AluOpType
ACT = mybir.ActivationFunctionType
AX = mybir.AxisListType

NB, S, D = 8, 128, 512
NC = D // 128
HEADS, HD = 32, 16
HC = 128 // HD
EXPERTS, RANK, RDIM = 64, 8, 16
TAPS, TOPK = 9, 16
SCALING = 32.0 / TOPK
EPS = 1e-5
LOW = -3.0e38
PICKED = -1.0e38

(FWD, FV, FVX, GV, GVX, GWD, CR1, CR2, EI1, EI2, OI1, OI2, IDENT) = range(13)
NMATS = 13
JORDER = [0, 2, 4, 6, 1, 3, 5, 7]


def decoder_layer(nc, x, ctx_in, wqkv, wo, a_t, b_t, wq_t, keys_t, mats, table, rank_l, rank_r, blockmask, ones_pad, identb, causal, out):
    st = ExitStack()
    with st:
        def sb(name, shape, dt=F32):
            return st.enter_context(nc.sbuf_tensor(name, shape, dt))

        def pb(name, dt=F32):
            return st.enter_context(nc.psum_tensor(name, [128, 512], dt))

        def sem(name):
            return st.enter_context(nc.semaphore(name))

        x_all = sb("x_all", [128, NB + 1, D])
        ctx_all = sb("ctx_all", [128, NB, D])
        mat = sb("mat", [128, NMATS, 128])
        w_qkv = sb("w_qkv", [128, NC, HEADS * HD + 2 * HD])
        w_krep = sb("w_krep", [128, NC, HC, HD])
        w_o = sb("w_o", [128, NC, D])
        w_a = sb("w_a", [128, NC, D])
        w_b = sb("w_b", [128, NC, D])
        w_rq = sb("w_rq", [128, NC, RDIM])
        w_keys = sb("w_keys", [RDIM, EXPERTS])
        tab = sb("tab", [128, NC, HC, S], BF16)
        rank_lhs = sb("rank_lhs", [128, 128], BF16)
        rank_rhs = sb("rank_rhs", [128, NC, HC, S], BF16)
        bmask = sb("bmask", [128, HC])
        onesp = sb("onesp", [128, 2, 32])
        idb = sb("idb", [128, 128], BF16)
        maskt = sb("maskt", [128, 128], BF16)
        half_neg = sb("half_neg", [128, 1])
        stats1 = sb("stats1", [128, 6]); mv1 = sb("mv1", [128, 2]); ve1 = sb("ve1", [128, 1]); rstd1 = sb("rstd1", [128, 1])
        xn = sb("xn", [128, D])
        xn_t = sb("xn_t", [128, NC, S])
        q_hi = sb("q_hi", [128, NC, S], F32R)
        q_lo = sb("q_lo", [128, NC, S], F32R)
        k_hi = sb("k_hi", [128, S], F32R)
        k_lo = sb("k_lo", [128, S])
        kb_hi = sb("kb_hi", [128, HC, S], F32R)
        kb_lo = sb("kb_lo", [128, HC, S], F32R)
        vpad = sb("vpad", [128, 2, 32])
        rowmax = sb("rowmax", [128, HEADS])
        nm_hi = sb("nm_hi", [HEADS, S], BF16)
        nm_lo = sb("nm_lo", [HEADS, S], BF16)
        probs = sb("probs", [128, HC, NC * S])
        rsum = sb("rsum", [128, D])
        attn_t = sb("attn_t", [128, D])
        stats2 = sb("stats2", [128, 6]); mv2 = sb("mv2", [128, 2]); ve2 = sb("ve2", [128, 1]); rstd2 = sb("rstd2", [128, 1])
        qn = sb("qn", [128, D])
        fv = sb("fv", [128, D]); fvx = sb("fvx", [128, D]); gv = sb("gv", [128, D]); gvx = sb("gvx", [128, D])
        pr1 = sb("pr1", [128, D]); pr2 = sb("pr2", [128, D])
        corr = sb("corr", [128, NC, S]); corr2 = sb("corr2", [128, NC, S]); corr3 = sb("corr3", [128, NC, S])
        top8 = sb("top8", [128, NC, 8]); next8 = sb("next8", [128, NC, 8]); ninth = sb("ninth", [128, NC, 8])
        negtop = sb("negtop", [128, NC])
        ecorr = sb("ecorr", [128, NC, S])
        wtap = sb("wtap", [128, NC, S]); wsum = sb("wsum", [128, NC]); wrec = sb("wrec", [128, NC])
        wtap_t = sb("wtap_t", [128, D])
        pe1 = sb("pe1", [128, D]); pe2 = sb("pe2", [128, D]); po1 = sb("po1", [128, D]); po2 = sb("po2", [128, D])
        stats3 = sb("stats3", [128, 6]); mv3 = sb("mv3", [128, 2]); ve3 = sb("ve3", [128, 1]); rstd3 = sb("rstd3", [128, 1])
        hn = sb("hn", [128, D])
        h_t = sb("h_t", [128, NC, S])
        rq_t = sb("rq_t", [RDIM, S])
        sc = sb("sc", [128, EXPERTS]); sc2 = sb("sc2", [128, EXPERTS]); sc3 = sb("sc3", [128, EXPERTS])
        st8a = sb("st8a", [128, 8]); st8b = sb("st8b", [128, 8]); negs = sb("negs", [128, 1])
        esc = sb("esc", [128, EXPERTS]); gate = sb("gate", [128, EXPERTS]); gsum = sb("gsum", [128, 1]); grec = sb("grec", [128, 1])
        gate2 = sb("gate2", [128, EXPERTS])
        zg = sb("zg", [128, D])
        zg_t = sb("zg_t", [128, NC, S])

        P = [pb(f"bank{i}") for i in range(8)]

        names = """held in_x0 in_x in_ctx in_mat in_wqkv in_wo in_wa in_wb in_wr in_small in_tab const_ready
            stat1 mvr1 vadd1 rstdr1 xn_ready xnT_ps xnT_ready q_ps qhi_ready qlo_ready kv_ps khi_ready klo_ready kb_ready v_ready
            ql_ps ql_max maxT_ps nmax_ready rank_ready kl_ps exp_ready pv_ps rsum_ready attn_ready wo_ps a_done
            stat2 mvr2 vadd2 rstdr2 qn_ready fq_ps fctx_ps fctx_ready pr_ready corr_ps corr_ready top_a top_b ecorr_ready wtap_step wtap_ready
            wT_ps wT_ready fw_ps pe_ready fwo_ps po_ready inv_ps b_done
            stat3 mvr3 vadd3 rstdr3 hn_ready hT_ps hT_ready z_ps rq_ps rq_ready sc_ps sc_ready top_c esc_ready gate_step zg_ready zgT_ps zgT_ready
            ffn_ps c_done out_done""".split()
        s = {n: sem(n) for n in names}

        def freed(eng, name, value):
            if not isinstance(value, int) or value > 0:
                eng.wait_ge(s[name], value)

        def hold(eng, name, value):
            eng.wait_ge(s[name], value)
            if not isinstance(value, int):
                eng.sem_inc(s["held"], 1)

        block = st.enter_context(nc.Block())

        def turns(eng, body):
            body(0, None, None)
            body(1, 0, None)
            body(2, 1, 0)
            with eng.Fori(3, NB) as i:
                body(i, i - 1, i - 2)
            body(None, NB - 1, NB - 2)
            body(None, None, NB - 1)

        @block.sync
        def _(sp):
            sp.dma_start(x_all[:, 0, :], x[0]).then_inc(s["in_x0"], 16)
            sp.dma_start(mat[:, :, :], mats).then_inc(s["in_mat"], 16)
            sp.dma_start(rank_lhs[:, :], rank_l).then_inc(s["in_small"], 16)
            sp.dma_start(rank_rhs[:, :, :, :], rank_r).then_inc(s["in_small"], 16)
            sp.dma_start(bmask[:, :], blockmask).then_inc(s["in_small"], 16)
            sp.dma_start(onesp[:, :, :], ones_pad).then_inc(s["in_small"], 16)
            sp.dma_start(idb[:, :], identb).then_inc(s["in_small"], 16)
            sp.dma_start(maskt[:, :], causal).then_inc(s["in_small"], 16)
            sp.dma_start(tab[:, :, :, :], table).then_inc(s["in_tab"], 16)
            sp.dma_start(x_all[:, 1:NB, :], x[1:NB].rearrange("b t d -> t b d")).then_inc(s["in_x"], 16)
            sp.dma_start(ctx_all[:, :, :], ctx_in.rearrange("b t d -> t b d")).then_inc(s["in_ctx"], 16)
            sp.dma_start(w_a[:, :, :], a_t.rearrange("(k p) n -> p k n", p=128)).then_inc(s["in_wa"], 16)
            sp.dma_start(w_rq[:, :, :], wq_t.rearrange("(k p) n -> p k n", p=128)).then_inc(s["in_wr"], 16)
            sp.dma_start(w_keys[:, :], keys_t).then_inc(s["in_wr"], 16)
            sp.dma_start(w_b[:, :, :], b_t.rearrange("(k p) n -> p k n", p=128)).then_inc(s["in_wb"], 16)

            def body(a, b, c):
                if a is not None:
                    hold(sp, "nmax_ready", a * 2 + 2)
                    freed(sp, "kl_ps", a * 8)
                    sp.dma_start(rank_rhs[3:4, :, :, :], nm_hi[:, :]).then_inc(s["rank_ready"], 16)
                    sp.dma_start(rank_rhs[4:5, :, :, :], nm_lo[:, :]).then_inc(s["rank_ready"], 16)
                if c is not None:
                    hold(sp, "c_done", c + 1)
                    sp.dma_start(out[bass.ds(c, 1)].rearrange("b t d -> (b t) d"), x_all[:, c, :]).then_inc(s["out_done"], 16)

            sp.wait_ge(s["in_small"], 16 * 6)
            turns(sp, body)
            sp.wait_ge(s["out_done"], 16 * NB)

        @block.gpsimd
        def _(pool):
            pool.memset(half_neg[:, :], -0.5).then_inc(s["const_ready"], 1)
            pool.memset(ninth[:, :, :], LOW).then_inc(s["const_ready"], 1)
            pool.memset(vpad[:, :, :], 0.0).then_inc(s["const_ready"], 1)
            pool.memset(x_all[:, NB, :], 0.0).then_inc(s["const_ready"], 1)
            pool.wait_ge(s["in_wqkv"], 16)
            for j in range(HC):
                pool.tensor_copy(w_krep[:, :, j, :], w_qkv[:, :, HEADS * HD:HEADS * HD + HD]).then_inc(s["const_ready"], 1)
            pool.wait_ge(s["const_ready"], 4 + HC)

            def rstd(n, mvr, vadd, rstdr, mv, ve, rs):
                hold(pool, mvr, n + 1)
                pool.tensor_scalar(ve[:, :], mv[:, 1:2], EPS, None, ALU.add).then_inc(s[vadd], 1)
                pool.wait_ge(s[vadd], n + 1)
                pool.tensor_tensor(rs[:, :], ve[:, :], half_neg[:, :], ALU.pow).then_inc(s[rstdr], 1)

            def body(a, b, c):
                if b is not None:
                    rstd(b, "mvr2", "vadd2", "rstdr2", mv2, ve2, rstd2)
                if c is not None:
                    rstd(c, "mvr3", "vadd3", "rstdr3", mv3, ve3, rstd3)
                if a is not None:
                    rstd(a + 1, "mvr1", "vadd1", "rstdr1", mv1, ve1, rstd1)

            rstd(0, "mvr1", "vadd1", "rstdr1", mv1, ve1, rstd1)
            turns(pool, body)

        @block.scalar
        def _(act):
            act.dma_start(w_qkv[:, :, :], wqkv.rearrange("(k p) n -> p k n", p=128)).then_inc(s["in_wqkv"], 16)
            act.dma_start(w_o[:, :, :], wo.rearrange("(k p) n -> p k n", p=128)).then_inc(s["in_wo"], 16)

            def copy(dst, src):
                return act.activation(dst, src, ACT.Copy)

            def body(a, b, c):
                if a is not None:
                    act.wait_ge(s["xnT_ps"], a + 1)
                    freed(act, "kv_ps", a)
                    copy(xn_t[:, :, :], P[2][:, :]).then_inc(s["xnT_ready"], 1)
                if c is not None:
                    act.wait_ge(s["hT_ps"], c + 1)
                    freed(act, "z_ps", c)
                    copy(h_t[:, :, :], P[6][:, :]).then_inc(s["hT_ready"], 1)
                if b is not None:
                    act.wait_ge(s["fctx_ps"], b * 4 + 1)
                    freed(act, "pe_ready", b)
                    copy(fv[:, :], P[5][:, :]).then_inc(s["fctx_ready"], 1)
                    act.wait_ge(s["fctx_ps"], b * 4 + 2)
                    copy(fvx[:, :], P[5][:, :]).then_inc(s["fctx_ready"], 1)
                if a is not None:
                    act.wait_ge(s["q_ps"], a + 1)
                    freed(act, "kl_ps", a * 8)
                    act.activation(q_hi[:, :, :], P[3][:, :], ACT.Copy, scale=HD ** -0.5).then_inc(s["qhi_ready"], 1)
                    act.wait_ge(s["kv_ps"], a + 1)
                    copy(k_hi[:, :], P[2][:, 0:S]).then_inc(s["khi_ready"], 1)
                if b is not None:
                    act.wait_ge(s["corr_ps"], b + 1)
                    freed(act, "wtap_step", b * 3)
                    copy(corr[:, :, :], P[4][:, :]).then_inc(s["corr_ready"], 1)
                if c is not None:
                    act.wait_ge(s["rq_ps"], c + 1)
                    copy(rq_t[:, :], P[6][0:RDIM, 0:S]).then_inc(s["rq_ready"], 1)
                if b is not None:
                    act.wait_ge(s["top_a"], b * 5 + 5)
                    act.wait_ge(s["corr_ready"], b + 1)
                    for n in range(NC):
                        act.activation(ecorr[:, n, :], corr[:, n, :], ACT.Exp, bias=negtop[:, n:n + 1]).then_inc(s["ecorr_ready"], 1)
                    freed(act, "po_ready", b)
                    act.wait_ge(s["fctx_ps"], b * 4 + 3)
                    copy(gv[:, :], P[5][:, :]).then_inc(s["fctx_ready"], 1)
                    act.wait_ge(s["fctx_ps"], b * 4 + 4)
                    copy(gvx[:, :], P[5][:, :]).then_inc(s["fctx_ready"], 1)
                if c is not None:
                    act.wait_ge(s["sc_ps"], c + 1)
                    copy(sc[:, :], P[6][:, 128:128 + EXPERTS]).then_inc(s["sc_ready"], 1)
                if b is not None:
                    act.wait_ge(s["wT_ps"], b + 1)
                    copy(wtap_t[:, :], P[4][:, :]).then_inc(s["wT_ready"], 1)
                if c is not None:
                    act.wait_ge(s["top_c"], c * 6 + 2)
                    act.activation(esc[:, :], sc[:, :], ACT.Exp, bias=negs[:, :]).then_inc(s["esc_ready"], 1)
                    act.wait_ge(s["zgT_ps"], c + 1)
                    copy(zg_t[:, :, :], P[6][:, :]).then_inc(s["zgT_ready"], 1)
                if a is not None:
                    freed(act, "pv_ps", a)
                    for n, j in enumerate(JORDER):
                        act.wait_ge(s["kl_ps"], a * 8 + n + 1)
                        act.activation(probs[:, j, :], P[n % 2][:, :], ACT.Exp).then_inc(s["exp_ready"], 1)

            turns(act, body)

        @block.vector
        def _(dve):
            def moments(n, src, stats, mv, stat, mvr):
                dve.bn_stats(stats[:, :], src).then_inc(s[stat], 1)
                hold(dve, stat, n + 1)
                dve.bn_aggr(mv[:, :], stats[:, :]).then_inc(s[mvr], 1)

            def normalize(n, dst, src, mv, rs, rstdr, ready):
                dve.wait_ge(s[rstdr], n + 1)
                dve.tensor_scalar(dst, src, mv[:, 0:1], rs[:, 0:1], ALU.subtract, ALU.mult).then_inc(s[ready], 1)

            def body(a, b, c):
                if b is not None:
                    dve.wait_ge(s["a_done"], b + 1)
                    moments(b, x_all[:, b, :], stats2, mv2, "stat2", "mvr2")
                if c is not None:
                    dve.wait_ge(s["b_done"], c + 1)
                    moments(c, x_all[:, c, :], stats3, mv3, "stat3", "mvr3")
                if b is not None:
                    normalize(b, qn[:, :], x_all[:, b, :], mv2, rstd2, "rstdr2", "qn_ready")
                if c is not None:
                    normalize(c, hn[:, :], x_all[:, c, :], mv3, rstd3, "rstdr3", "hn_ready")
                if b is not None:
                    dve.wait_ge(s["fq_ps"], b + 1)
                    dve.wait_ge(s["fctx_ready"], b * 4 + 1)
                    dve.tensor_tensor(pr1[:, :], P[4][:, :], fv[:, :], ALU.mult).then_inc(s["pr_ready"], 1)
                    dve.wait_ge(s["fctx_ready"], b * 4 + 2)
                    dve.tensor_tensor(pr2[:, :], P[4][:, :], fvx[:, :], ALU.mult).then_inc(s["pr_ready"], 1)
                if a is not None:
                    dve.wait_ge(s["qhi_ready"], a + 1)
                    dve.scalar_tensor_tensor(out=q_lo[:, :, :], in0=P[3][:, :].rearrange("p (c t) -> p c t", c=NC), scalar=HD ** -0.5,
                                             in1=q_hi[:, :, :].bitcast(F32), op0=ALU.mult, op1=ALU.subtract).then_inc(s["qlo_ready"], 1)
                    dve.wait_ge(s["khi_ready"], a + 1)
                    dve.tensor_tensor(k_lo[:, :], P[2][:, 0:S], k_hi[:, :].bitcast(F32), ALU.subtract).then_inc(s["klo_ready"], 1)
                    for par in range(2):
                        dve.tensor_copy(vpad[:, par, HD * par:HD * par + HD], P[2][:, S:S + HD]).then_inc(s["v_ready"], 1)
                    mask_b = bmask[:, :].rearrange("p (j o) -> p j o", o=1).broadcast_to([128, HC, S])
                    dve.tensor_tensor(kb_hi[:, :, :], k_hi[:, :].bitcast(F32).rearrange("p (o t) -> p o t", o=1).broadcast_to([128, HC, S]),
                                      mask_b, ALU.mult).then_inc(s["kb_ready"], 1)
                    dve.wait_ge(s["klo_ready"], a + 1)
                    dve.tensor_tensor(kb_lo[:, :, :], k_lo[:, :].rearrange("p (o t) -> p o t", o=1).broadcast_to([128, HC, S]),
                                      mask_b, ALU.mult).then_inc(s["kb_ready"], 1)
                if b is not None:
                    hold(dve, "corr_ready", b + 1)
                    for n in range(NC):
                        dve.max(top8[:, n, :], corr[:, n, :]).then_inc(s["top_a"], 1)
                    dve.wait_ge(s["top_a"], b * 5 + 4)
                    dve.tensor_scalar(negtop[:, :], top8[:, :, 0], -1.0, None, ALU.mult).then_inc(s["top_a"], 1)
                    for n in range(NC):
                        dve.match_replace(corr2[:, n, :], top8[:, n, :], corr[:, n, :], LOW).then_inc(s["top_b"], 1)
                    for n in range(NC):
                        hold(dve, "top_b", b * 13 + n + 1)
                        dve.max(next8[:, n, :], corr2[:, n, :]).then_inc(s["top_b"], 1)
                    dve.wait_ge(s["top_b"], b * 13 + 8)
                    dve.tensor_copy(ninth[:, :, 0], next8[:, :, 0]).then_inc(s["top_b"], 1)
                    hold(dve, "top_b", b * 13 + 9)
                    for n in range(NC):
                        dve.match_replace(corr3[:, n, :], ninth[:, n, :], corr2[:, n, :], LOW).then_inc(s["top_b"], 1)
                    dve.wait_ge(s["top_b"], b * 13 + 13)
                    dve.wait_ge(s["ecorr_ready"], b * 4 + 4)
                    dve.scalar_tensor_tensor(out=wtap[:, :, :], in0=corr3[:, :, :], scalar=PICKED, in1=ecorr[:, :, :],
                                             op0=ALU.is_lt, op1=ALU.mult).then_inc(s["wtap_step"], 1)
                    dve.wait_ge(s["wtap_step"], b * 3 + 1)
                    dve.tensor_reduce(wsum[:, :], wtap[:, :, :], AX.X, ALU.add).then_inc(s["wtap_step"], 1)
                    dve.wait_ge(s["wtap_step"], b * 3 + 2)
                    dve.reciprocal(wrec[:, :], wsum[:, :]).then_inc(s["wtap_step"], 1)
                    dve.wait_ge(s["wtap_step"], b * 3 + 3)
                    dve.tensor_tensor(wtap[:, :, :], wtap[:, :, :], wrec[:, :].rearrange("p (n o) -> p n o", o=1).broadcast_to([128, NC, S]),
                                      ALU.mult).then_inc(s["wtap_ready"], 1)
                if c is not None:
                    hold(dve, "sc_ready", c + 1)
                    dve.max(st8a[:, :], sc[:, :]).then_inc(s["top_c"], 1)
                    dve.wait_ge(s["top_c"], c * 6 + 1)
                    dve.tensor_scalar(negs[:, :], st8a[:, 0:1], -1.0, None, ALU.mult).then_inc(s["top_c"], 1)
                    dve.match_replace(sc2[:, :], st8a[:, :], sc[:, :], LOW).then_inc(s["top_c"], 1)
                    hold(dve, "top_c", c * 6 + 3)
                    dve.max(st8b[:, :], sc2[:, :]).then_inc(s["top_c"], 1)
                    hold(dve, "top_c", c * 6 + 4)
                    dve.match_replace(sc3[:, :], st8b[:, :], sc2[:, :], LOW).then_inc(s["top_c"], 1)
                    dve.wait_ge(s["top_c"], c * 6 + 5)
                    dve.wait_ge(s["esc_ready"], c + 1)
                    dve.scalar_tensor_tensor(out=gate[:, :], in0=sc3[:, :], scalar=PICKED, in1=esc[:, :], op0=ALU.is_lt, op1=ALU.mult,
                                             ).then_inc(s["top_c"], 1)
                    dve.wait_ge(s["top_c"], c * 6 + 6)
                    dve.tensor_reduce(gsum[:, :], gate[:, :], AX.X, ALU.add).then_inc(s["gate_step"], 1)
                    dve.wait_ge(s["gate_step"], c * 3 + 1)
                    dve.reciprocal(grec[:, :], gsum[:, :]).then_inc(s["gate_step"], 1)
                    dve.wait_ge(s["gate_step"], c * 3 + 2)
                    dve.tensor_scalar(gate2[:, :], gate[:, :], grec[:, :], SCALING, ALU.mult, ALU.mult).then_inc(s["gate_step"], 1)
                    dve.wait_ge(s["gate_step"], c * 3 + 3)
                    dve.wait_ge(s["z_ps"], c + 1)
                    dve.tensor_tensor(zg[:, :].rearrange("p (e r) -> p e r", r=RANK), P[7][:, :].rearrange("p (e r) -> p e r", r=RANK),
                                      gate2[:, :].rearrange("p (e o) -> p e o", o=1).broadcast_to([128, EXPERTS, RANK]), ALU.mult).then_inc(s["zg_ready"], 1)
                if b is not None:
                    dve.wait_ge(s["fw_ps"], b + 1)
                    dve.tensor_tensor(pe1[:, :], P[4][:, :], fv[:, :], ALU.mult)
                    dve.tensor_tensor(pe2[:, :], P[4][:, :], fvx[:, :], ALU.mult).then_inc(s["pe_ready"], 1)
                    dve.wait_ge(s["fwo_ps"], b + 1)
                    dve.wait_ge(s["fctx_ready"], b * 4 + 4)
                    dve.tensor_tensor(po1[:, :], P[5][:, :], gv[:, :], ALU.mult)
                    dve.tensor_tensor(po2[:, :], P[5][:, :], gvx[:, :], ALU.mult).then_inc(s["po_ready"], 1)
                if a is not None:
                    for n in range(8):
                        dve.wait_ge(s["ql_ps"], a * 8 + n + 1)
                        dve.tensor_reduce(rowmax[:, 4 * n:4 * n + 4], P[n % 2][:, :].rearrange("p (j k) -> p j k", k=S), AX.X, ALU.max).then_inc(s["ql_max"], 1)
                    dve.wait_ge(s["maxT_ps"], a + 1)
                    freed(dve, "rank_ready", a * 32)
                    dve.tensor_scalar(nm_hi[:, :], P[2][0:HEADS, 0:S], -1.0, None, ALU.mult).then_inc(s["nmax_ready"], 1)
                    dve.wait_ge(s["nmax_ready"], a * 2 + 1)
                    dve.scalar_tensor_tensor(out=nm_lo[:, :], in0=P[2][0:HEADS, 0:S], scalar=-1.0, in1=nm_hi[:, :],
                                             op0=ALU.mult, op1=ALU.subtract).then_inc(s["nmax_ready"], 1)
                if c is not None:
                    dve.wait_ge(s["ffn_ps"], c + 1)
                    dve.tensor_tensor(x_all[:, c, :], x_all[:, c, :], P[7][:, :], ALU.add).then_inc(s["c_done"], 1)
                if b is not None:
                    dve.wait_ge(s["inv_ps"], b + 1)
                    dve.tensor_tensor(x_all[:, b, :], x_all[:, b, :], P[4][:, :], ALU.add).then_inc(s["b_done"], 1)
                if a is not None:
                    nxt = a + 1
                    first_next(nxt, a)
                    dve.wait_ge(s["pv_ps"], a + 1)
                    dve.reciprocal(rsum[:, :], P[3][:, :]).then_inc(s["rsum_ready"], 1)
                    dve.wait_ge(s["rsum_ready"], a + 1)
                    dve.tensor_tensor(attn_t[:, :], P[2][:, :], rsum[:, :], ALU.mult).then_inc(s["attn_ready"], 1)
                    dve.wait_ge(s["wo_ps"], a + 1)
                    dve.tensor_tensor(x_all[:, a, :], x_all[:, a, :], P[3][:, :], ALU.add).then_inc(s["a_done"], 1)

            def first_next(nxt, a):
                src = x_all[:, nxt, :]
                moments(nxt, src, stats1, mv1, "stat1", "mvr1")
                freed(dve, "xnT_ps", nxt)
                normalize(nxt, xn[:, :], src, mv1, rstd1, "rstdr1", "xn_ready")

            dve.wait_ge(s["in_x0"], 16)
            dve.wait_ge(s["const_ready"], 4 + HC)
            moments(0, x_all[:, 0, :], stats1, mv1, "stat1", "mvr1")
            normalize(0, xn[:, :], x_all[:, 0, :], mv1, rstd1, "rstdr1", "xn_ready")
            dve.wait_ge(s["in_small"], 16 * 6)
            dve.wait_ge(s["in_x"], 16)
            turns(dve, body)

        @block.tensor
        def _(pe):
            ident = mat[:, IDENT, :]

            def transposes(bank, src, signal):
                for n in range(NC):
                    last = pe.transpose(P[bank][:, n * 128:(n + 1) * 128], src[:, n * 128:(n + 1) * 128], ident)
                last.then_inc(s[signal], 1)

            def body(a, b, c):
                if a is not None:
                    pe.wait_ge(s["xn_ready"], a + 1)
                    freed(pe, "attn_ready", a)
                    transposes(2, xn[:, :], "xnT_ps")
                if c is not None:
                    pe.wait_ge(s["hn_ready"], c + 1)
                    freed(pe, "zgT_ready", c)
                    transposes(6, hn[:, :], "hT_ps")
                if b is not None:
                    freed(pe, "po_ready", b)
                    pe.matmul(P[5][:, :], mat[:, FV, :], ctx_all[:, b, :], start=True, stop=True).then_inc(s["fctx_ps"], 1)
                    pe.wait_ge(s["qn_ready"], b + 1)
                    freed(pe, "b_done", b)
                    pe.matmul(P[4][:, :], mat[:, FWD, :], qn[:, :], start=True, stop=True).then_inc(s["fq_ps"], 1)
                    pe.wait_ge(s["fctx_ready"], b * 4 + 1)
                    pe.matmul(P[5][:, :], mat[:, FVX, :], ctx_all[:, b, :], start=True, stop=True).then_inc(s["fctx_ps"], 1)
                if a is not None:
                    pe.wait_ge(s["xnT_ready"], a + 1)
                    freed(pe, "a_done", a)
                    for n in range(NC):
                        for k in range(NC):
                            last = pe.matmul(P[3][:, n * S:(n + 1) * S], w_qkv[:, k, n * 128:(n + 1) * 128], xn_t[:, k, :],
                                             start=(k == 0), stop=(k == NC - 1))
                    last.then_inc(s["q_ps"], 1)
                    for k in range(NC):
                        pe.matmul(P[2][:, 0:S], w_krep[:, k, :, :], xn_t[:, k, :], start=(k == 0), stop=(k == NC - 1))
                    for k in range(NC):
                        last = pe.matmul(P[2][:, S:S + HD], xn_t[:, k, :], w_qkv[:, k, HEADS * HD + HD:], start=(k == 0), stop=(k == NC - 1))
                    last.then_inc(s["kv_ps"], 1)
                if b is not None:
                    pe.wait_ge(s["pr_ready"], b * 2 + 2)
                    for n in range(NC):
                        ch = slice(n * 128, (n + 1) * 128)
                        pe.matmul(P[4][:, ch], pr1[:, ch], mat[:, CR1, :], start=True, stop=False)
                        last = pe.matmul(P[4][:, ch], pr2[:, ch], mat[:, CR2, :], start=False, stop=True)
                    last.then_inc(s["corr_ps"], 1)
                if c is not None:
                    pe.wait_ge(s["hT_ready"], c + 1)
                    freed(pe, "c_done", c)
                    for k in range(NC):
                        last = pe.matmul(P[6][0:RDIM, 0:S], w_rq[:, k, :], h_t[:, k, :], start=(k == 0), stop=(k == NC - 1))
                    last.then_inc(s["rq_ps"], 1)
                    for k in range(NC):
                        last = pe.matmul(P[7][:, :], h_t[:, k, :], w_a[:, k, :], start=(k == 0), stop=(k == NC - 1))
                    last.then_inc(s["z_ps"], 1)
                if b is not None:
                    pe.wait_ge(s["fctx_ready"], b * 4 + 2)
                    pe.matmul(P[5][:, :], mat[:, GV, :], ctx_all[:, b, :], start=True, stop=True).then_inc(s["fctx_ps"], 1)
                if c is not None:
                    pe.wait_ge(s["rq_ready"], c + 1)
                    pe.matmul(P[6][:, 128:128 + EXPERTS], rq_t[:, :], w_keys[:, :], start=True, stop=True).then_inc(s["sc_ps"], 1)
                if b is not None:
                    pe.wait_ge(s["fctx_ready"], b * 4 + 3)
                    pe.matmul(P[5][:, :], mat[:, GVX, :], ctx_all[:, b, :], start=True, stop=True).then_inc(s["fctx_ps"], 1)
                    pe.wait_ge(s["wtap_ready"], b + 1)
                    transposes(4, wtap[:, :, :].rearrange("p n t -> p (n t)"), "wT_ps")
                    pe.wait_ge(s["wT_ready"], b + 1)
                    pe.matmul(P[4][:, :], mat[:, FWD, :], wtap_t[:, :], start=True, stop=True).then_inc(s["fw_ps"], 1)
                    pe.wait_ge(s["fctx_ready"], b * 4 + 4)
                    pe.matmul(P[5][:, :], mat[:, GWD, :], wtap_t[:, :], start=True, stop=True).then_inc(s["fwo_ps"], 1)
                if a is not None:
                    pe.wait_ge(s["kb_ready"], a * 2 + 1)
                    for n in range(8):
                        if n >= 2:
                            pe.wait_ge(s["ql_max"], a * 8 + n - 1)
                        ch, hf = n // 2, n % 2
                        pe.matmul(P[n % 2][:, :], q_hi[:, ch, :], kb_hi[:, 4 * hf:4 * hf + 4, :], start=True, stop=False)
                        pe.matmul(P[n % 2][:, :], idb[:, :], tab[:, ch, 4 * hf:4 * hf + 4, :], start=False, stop=True).then_inc(s["ql_ps"], 1)
                if c is not None:
                    pe.wait_ge(s["zg_ready"], c + 1)
                    transposes(6, zg[:, :], "zgT_ps")
                if a is not None:
                    pe.wait_ge(s["v_ready"], a * 2 + 2)
                    pe.wait_ge(s["ql_max"], a * 8 + 8)
                    pe.transpose(P[2][0:HEADS, 0:S], rowmax[:, :], ident).then_inc(s["maxT_ps"], 1)
                if b is not None:
                    pe.wait_ge(s["pe_ready"], b + 1)
                    pe.matmul(P[4][:, :], mat[:, EI1, :], pe1[:, :], start=True, stop=False)
                    pe.matmul(P[4][:, :], mat[:, EI2, :], pe2[:, :], start=False, stop=False)
                    pe.wait_ge(s["po_ready"], b + 1)
                    pe.matmul(P[4][:, :], mat[:, OI1, :], po1[:, :], start=False, stop=False)
                    pe.matmul(P[4][:, :], mat[:, OI2, :], po2[:, :], start=False, stop=True).then_inc(s["inv_ps"], 1)
                if c is not None:
                    pe.wait_ge(s["zgT_ready"], c + 1)
                    for k in range(NC):
                        last = pe.matmul(P[7][:, :], zg_t[:, k, :], w_b[:, k, :], start=(k == 0), stop=(k == NC - 1))
                    last.then_inc(s["ffn_ps"], 1)
                if a is not None:
                    pe.wait_ge(s["qlo_ready"], a + 1)
                    pe.wait_ge(s["kb_ready"], a * 2 + 2)
                    pe.wait_ge(s["rank_ready"], a * 32 + 32)
                    for n, j in enumerate(JORDER):
                        if n >= 2:
                            pe.wait_ge(s["exp_ready"], a * 8 + n - 1)
                        pe.matmul(P[n % 2][:, :], kb_hi[:, j, :], q_hi[:, :, :], start=True, stop=False)
                        pe.matmul(P[n % 2][:, :], kb_lo[:, j, :], q_hi[:, :, :], start=False, stop=False)
                        pe.matmul(P[n % 2][:, :], kb_hi[:, j, :], q_lo[:, :, :], start=False, stop=False)
                        pe.matmul(P[n % 2][:, :], maskt[:, :], idb[:, :].rearrange("p (o t) -> p o t", o=1).broadcast_to([128, NC, S]),
                                  start=False, stop=False)
                        pe.matmul(P[n % 2][:, :], rank_lhs[:, :], rank_rhs[:, :, j, :], start=False, stop=True).then_inc(s["kl_ps"], 1)
                    for half in range(2):
                        pe.wait_ge(s["exp_ready"], a * 8 + 4 * half + 4)
                        for bank, lhs in ((2, vpad), (3, onesp)):
                            for j in JORDER[4 * half:4 * half + 4]:
                                g = 32 * (j // 2)
                                last = pe.matmul(P[bank][g:g + 32, :], lhs[:, j % 2, :], probs[:, j, :], start=(half == 0), stop=(half == 1))
                    last.then_inc(s["pv_ps"], 1)
                    pe.wait_ge(s["attn_ready"], a + 1)
                    for k in range(NC):
                        last = pe.matmul(P[3][:, :], attn_t[:, k * 128:(k + 1) * 128], w_o[:, k, :], start=(k == 0), stop=(k == NC - 1))
                    last.then_inc(s["wo_ps"], 1)

            pe.wait_ge(s["in_mat"], 16)
            pe.wait_ge(s["in_wqkv"], 16)
            pe.wait_ge(s["const_ready"], 4 + HC)
            pe.wait_ge(s["in_tab"], 16)
            pe.wait_ge(s["in_small"], 16 * 6)
            pe.wait_ge(s["in_wo"], 16)
            pe.wait_ge(s["in_ctx"], 16)
            pe.wait_ge(s["in_wa"], 16)
            pe.wait_ge(s["in_wb"], 16)
            pe.wait_ge(s["in_wr"], 32)
            turns(pe, body)


def _constants():
    import numpy as np
    L, hlf = S, S // 2
    t = np.arange(L)[:, None].astype(np.float64)
    f = np.arange(hlf)[None, :].astype(np.float64)
    we, wo_ = 2 * np.pi * f / L, 2 * np.pi * (f + 0.5) / L
    fwd = np.concatenate([np.cos(we * t), -np.sin(we * t)], 1)
    fwd[:, hlf] = np.cos(np.pi * t[:, 0])
    swap = np.concatenate([fwd[:, hlf:], fwd[:, :hlf]], 1)
    swap[:, 0] = 1.0
    swap[:, hlf] = 0.0
    fv = fwd.copy()
    fv[L - 1, 0] += L
    gwd = np.concatenate([np.cos(wo_ * t), -np.sin(wo_ * t)], 1)
    gv = gwd.copy()
    gv[L - 1] -= gwd.sum(0)
    gvx = np.concatenate([gv[:, hlf:], gv[:, :hlf]], 1)
    tt = t.T
    ce, se = 2 * np.cos(we.T * tt) / L, 2 * np.sin(we.T * tt) / L
    base1 = np.concatenate([ce, ce], 0)
    base1[hlf] = np.cos(np.pi * tt[0]) / L
    cr1 = base1.copy()
    cr1[0] = 0.0
    cr2 = np.concatenate([se, -se], 0)
    cr2[0] = 1.0 / L
    cr2[hlf] = 0.0
    ei1 = base1.copy()
    ei1[0] = 1.0 / L
    ei2 = np.concatenate([-se, se], 0)
    ei2[0] = 0.0
    ei2[hlf] = 0.0
    co, so = 2 * np.cos(wo_.T * tt) / L, 2 * np.sin(wo_.T * tt) / L
    oi1 = np.concatenate([co, co], 0)
    oi2 = np.concatenate([-so, so], 0)
    mats = np.stack([fwd, fv, swap, gv, gvx, gwd, cr1, cr2, ei1 / 2, ei2 / 2, oi1 / 2, oi2 / 2, np.eye(L)], 1).astype(np.float32)
    bf = mybir.dt.np(BF16)
    slopes = ((2.0 ** (-2.0 ** (-(np.log2(HEADS) - 3)))) ** np.arange(1, HEADS + 1)).astype(np.float32)
    pos = np.arange(S)
    table = slopes.reshape(1, NC, HC, 1) * pos.reshape(1, 1, 1, S).astype(np.float32)
    table = np.where(pos.reshape(1, 1, 1, S) > pos.reshape(S, 1, 1, 1), np.float32(-1e30), table).astype(bf)
    rank_l = np.zeros((128, 128), bf)
    rank_l[0:3] = pos.astype(bf)
    rank_l[3:5] = 1.0
    rank_r = np.zeros((128, NC, HC, S), bf)
    rest = slopes.copy()
    for n in range(3):
        part = rest.astype(bf)
        rank_r[n] = part.reshape(NC, HC, 1)
        rest = rest - part.astype(np.float32)
    blockmask = (np.arange(128)[:, None] // HD == np.arange(HC)[None, :]).astype(np.float32)
    ones_pad = np.zeros((128, 2, 32), np.float32)
    ones_pad[:, 0, :HD] = 1.0
    ones_pad[:, 1, HD:] = 1.0
    return {"mats": mats, "table": table, "rank_l": rank_l, "rank_r": rank_r, "blockmask": blockmask, "ones_pad": ones_pad,
            "identb": np.eye(128).astype(bf), "causal": np.where(pos[None, :] > pos[:, None], np.float32(-1e30), np.float32(0)).astype(bf)}


def kernel(x, ctx_4096, L0_attn_Wqkv, L0_attn_Wo, L0_ffn_A_w, L0_ffn_B_w, L0_ffn_Wq_w, L0_ffn_keys):
    import numpy as np
    import concourse.bacc as bacc
    from concourse.bass_utils import run_bass_kernel_spmd

    nc = bacc.Bacc("TRN2", target_bir_lowering=False, num_devices=1)
    arrays = {
        "x": x, "ctx": ctx_4096, "wqkv": L0_attn_Wqkv, "wo": L0_attn_Wo, "a_t": np.asarray(L0_ffn_A_w).T,
        "b_t": np.asarray(L0_ffn_B_w).T, "wq_t": np.asarray(L0_ffn_Wq_w).T, "keys_t": np.asarray(L0_ffn_keys).T,
        **_constants(),
    }
    arrays = {f"in_{n}": np.ascontiguousarray(v) for n, v in arrays.items()}
    args = [nc.dram_tensor(n, v.shape, mybir.dt.from_np(v.dtype), kind="ExternalInput").ap() for n, v in arrays.items()]
    out = nc.dram_tensor("out", (NB, S, D), F32, kind="ExternalOutput").ap()
    decoder_layer(nc, *args, out)
    r = run_bass_kernel_spmd(nc, [arrays], core_ids=[0])
    return r.results[0]["out"]
```

```python
from contextlib import ExitStack

import concourse.bass as bass
from concourse import mybir

F32 = mybir.dt.float32
F32R = mybir.dt.float32r
BF16 = mybir.dt.bfloat16
ALU = mybir.AluOpType
ACT = mybir.ActivationFunctionType
AX = mybir.AxisListType

NB, S, D = 8, 128, 512
NC = D // 128
HEADS, HD = 32, 16
HC = 128 // HD
EXPERTS, RANK, RDIM = 64, 8, 16
TAPS, TOPK = 9, 16
SCALING = 32.0 / TOPK
EPS = 1e-5
LOW = -3.0e38
PICKED = -1.0e38

(FWD, FV, FVX, GV, GVX, GWD, CR1, CR2, EI1, EI2, OI1, OI2, IDENT) = range(13)
NMATS = 13
NCONST = 5
WT_AT = 4
JORDER = [0, 2, 4, 6, 1, 3, 5, 7]


def decoder_layer(nc, x, ctx_in, wqkv, wo, a_t, b_t, wq_t, keys_t, mats, table, rank_l, rank_r, blockmask, ones_pad, identb, causal, out):
    st = ExitStack()
    with st:
        def sb(name, shape, dt=F32):
            return st.enter_context(nc.sbuf_tensor(name, shape, dt))

        def pb(name, dt=F32):
            return st.enter_context(nc.psum_tensor(name, [128, 512], dt))

        def sem(name):
            return st.enter_context(nc.semaphore(name))

        x_all = sb("x_all", [128, NB + 1, D])
        ctx_all = sb("ctx_all", [128, NB, D])
        mat = sb("mat", [128, NMATS, 128])
        w_qkv = sb("w_qkv", [128, NC, HEADS * HD + 2 * HD])
        w_krep = sb("w_krep", [128, NC, HC, HD])
        w_o = sb("w_o", [128, NC, D])
        w_a = sb("w_a", [128, NC, D])
        w_b = sb("w_b", [128, NC, D])
        w_rq = sb("w_rq", [128, NC, RDIM])
        w_keys = sb("w_keys", [RDIM, EXPERTS])
        tab = sb("tab", [128, NC, HC, S], BF16)
        rank_lhs = sb("rank_lhs", [128, 128], BF16)
        rank_rhs = sb("rank_rhs", [128, NC, HC, S], BF16)
        bmask = sb("bmask", [128, HC])
        onesp = sb("onesp", [128, 2, 32])
        idb = sb("idb", [128, 128], BF16)
        maskt = sb("maskt", [128, 128], BF16)
        half_neg = sb("half_neg", [128, 1])
        stats1 = sb("stats1", [128, 6]); mv1 = sb("mv1", [128, 2]); ve1 = sb("ve1", [128, 1]); rstd1 = sb("rstd1", [128, 1])
        xn = sb("xn", [128, D])
        xn_t = sb("xn_t", [128, NC, S])
        q_hi = sb("q_hi", [128, NC, S], F32R)
        q_lo = sb("q_lo", [128, NC, S], F32R)
        k_hi = sb("k_hi", [128, S], F32R)
        k_lo = sb("k_lo", [128, S])
        kb_hi = sb("kb_hi", [128, HC, S], F32R)
        kb_lo = sb("kb_lo", [128, HC, S], F32R)
        vpad = sb("vpad", [128, 2, 32])
        rowmax = sb("rowmax", [128, HEADS])
        nm_hi = sb("nm_hi", [HEADS, S], BF16)
        nm_lo = sb("nm_lo", [HEADS, S], BF16)
        probs = sb("probs", [128, HC, NC * S])
        rsum = sb("rsum", [128, D])
        attn_t = sb("attn_t", [128, D])
        stats2 = sb("stats2", [128, 6]); mv2 = sb("mv2", [128, 2]); ve2 = sb("ve2", [128, 1]); rstd2 = sb("rstd2", [128, 1])
        qn = sb("qn", [128, D])
        fv = sb("fv", [128, D]); fvx = sb("fvx", [128, D]); gv = sb("gv", [128, D]); gvx = sb("gvx", [128, D])
        pr1 = sb("pr1", [128, D]); pr2 = sb("pr2", [128, D])
        corr = sb("corr", [128, NC, S]); corr2 = sb("corr2", [128, NC, S]); corr3 = sb("corr3", [128, NC, S])
        top8 = sb("top8", [128, NC, 8]); next8 = sb("next8", [128, NC, 8]); ninth = sb("ninth", [128, NC, 8])
        negtop = sb("negtop", [128, NC])
        ecorr = sb("ecorr", [128, NC, S])
        wtap = sb("wtap", [128, NC, S]); wsum = sb("wsum", [128, NC]); wrec = sb("wrec", [128, NC])
        wtap_t = sb("wtap_t", [128, D])
        pe1 = sb("pe1", [128, D]); pe2 = sb("pe2", [128, D]); po1 = sb("po1", [128, D]); po2 = sb("po2", [128, D])
        stats3 = sb("stats3", [128, 6]); mv3 = sb("mv3", [128, 2]); ve3 = sb("ve3", [128, 1]); rstd3 = sb("rstd3", [128, 1])
        hn = sb("hn", [128, D])
        h_t = sb("h_t", [128, NC, S])
        rq_t = sb("rq_t", [RDIM, S])
        sc = sb("sc", [128, EXPERTS]); sc2 = sb("sc2", [128, EXPERTS]); sc3 = sb("sc3", [128, EXPERTS])
        st8a = sb("st8a", [128, 8]); st8b = sb("st8b", [128, 8]); negs = sb("negs", [128, 1])
        esc = sb("esc", [128, EXPERTS]); gate = sb("gate", [128, EXPERTS]); gsum = sb("gsum", [128, 1]); grec = sb("grec", [128, 1])
        gate2 = sb("gate2", [128, EXPERTS])
        zg = sb("zg", [128, D])
        zg_t = sb("zg_t", [128, NC, S])

        P = [pb(f"bank{i}") for i in range(8)]

        names = """held krep_ready in_ident in_ctx0 in_rank in_x0 in_x in_ctx in_mat in_wqkv in_wo in_wa in_wb in_wr in_small in_tab const_ready
            stat1 mvr1 vadd1 rstdr1 xn_ready xnT_ps xnT_ready q_ps qhi_ready qlo_ready kv_ps khi_ready klo_ready kb_ready v_ready
            ql_ps ql_max maxT_ps nmax_ready rank_ready kl_ps exp_ready pv_ps rsum_ready attn_ready wo_ps a_done
            stat2 mvr2 vadd2 rstdr2 qn_ready fq_ps fctx_ps fctx_ready pr_ready corr_ps corr_ready top_a top_b ecorr_ready wtap_step wtap_ready
            wT_ps wT_ready fw_ps pe_ready fwo_ps po_ready inv_ps b_done
            stat3 mvr3 vadd3 rstdr3 hn_ready hT_ps hT_ready z_ps rq_ps rq_ready sc_ps sc_ready top_c esc_ready gate_step zg_ready zgT_ps zgT_ready
            ffn_ps c_done out_done""".split()
        s = {n: sem(n) for n in names}

        def freed(eng, name, value):
            if not isinstance(value, int) or value > 0:
                eng.wait_ge(s[name], value)

        def hold(eng, name, value):
            eng.wait_ge(s[name], value)
            if not isinstance(value, int):
                eng.sem_inc(s["held"], 1)

        block = st.enter_context(nc.Block())

        def turns(eng, body):
            body(0, None, None)
            body(1, 0, None)
            body(2, 1, 0)
            with eng.Fori(3, NB) as i:
                body(i, i - 1, i - 2)
            body(None, NB - 1, NB - 2)
            body(None, None, NB - 1)

        @block.sync
        def _(sp):
            sp.dma_start(x_all[:, 0, :], x[0]).then_inc(s["in_x0"], 16)
            sp.dma_start(mat[:, IDENT, :], mats[:, IDENT, :]).then_inc(s["in_ident"], 16)
            sp.dma_start(w_qkv[:, :, :], wqkv.rearrange("(k p) n -> p k n", p=128)).then_inc(s["in_wqkv"], 16)
            sp.dma_start(bmask[:, :], blockmask).then_inc(s["in_small"], 16)
            sp.dma_start(idb[:, :], identb).then_inc(s["in_small"], 16)
            sp.dma_start(tab[:, :, :, :], table).then_inc(s["in_tab"], 16)
            sp.dma_start(rank_lhs[:, :], rank_l).then_inc(s["in_rank"], 16)
            sp.dma_start(maskt[:, :], causal).then_inc(s["in_rank"], 16)
            sp.wait_ge(s["const_ready"], NCONST)
            sp.dma_start(rank_rhs[0:3, :, :, :], rank_r).then_inc(s["in_rank"], 16)
            sp.dma_start(onesp[:, :, :], ones_pad).then_inc(s["in_rank"], 16)
            sp.dma_start(mat[:, 0:IDENT, :], mats[:, 0:IDENT, :]).then_inc(s["in_mat"], 16)
            sp.dma_start(ctx_all[:, 0, :], ctx_in[0]).then_inc(s["in_ctx0"], 16)
            sp.dma_start(w_o[:, :, :], wo.rearrange("(k p) n -> p k n", p=128)).then_inc(s["in_wo"], 16)
            sp.dma_start(x_all[:, 1:NB, :], x[1:NB].rearrange("b t d -> t b d")).then_inc(s["in_x"], 16)
            sp.dma_start(ctx_all[:, 1:NB, :], ctx_in[1:NB].rearrange("b t d -> t b d")).then_inc(s["in_ctx"], 16)
            sp.dma_start(w_rq[:, :, :], wq_t.rearrange("(k p) n -> p k n", p=128)).then_inc(s["in_wr"], 16)
            sp.dma_start(w_keys[:, :], keys_t).then_inc(s["in_wr"], 16)
            sp.dma_start(w_a[:, :, :], a_t.rearrange("(k p) n -> p k n", p=128)).then_inc(s["in_wa"], 16)
            sp.dma_start(w_b[:, :, :], b_t.rearrange("(k p) n -> p k n", p=128)).then_inc(s["in_wb"], 16)

            def body(a, b, c):
                if a is not None:
                    hold(sp, "nmax_ready", a * 2 + 2)
                    freed(sp, "kl_ps", a * 8)
                    sp.dma_start(rank_rhs[3:4, :, :, :], nm_hi[:, :]).then_inc(s["rank_ready"], 16)
                    sp.dma_start(rank_rhs[4:5, :, :, :], nm_lo[:, :]).then_inc(s["rank_ready"], 16)
                if c is not None:
                    hold(sp, "c_done", c + 1)
                    sp.dma_start(out[bass.ds(c, 1)].rearrange("b t d -> (b t) d"), x_all[:, c, :]).then_inc(s["out_done"], 16)

            turns(sp, body)
            sp.wait_ge(s["out_done"], 16 * NB)

        @block.gpsimd
        def _(pool):
            pool.memset(half_neg[:, :], -0.5).then_inc(s["const_ready"], 1)
            pool.memset(ninth[:, :, :], LOW).then_inc(s["const_ready"], 1)
            pool.memset(vpad[:, :, :], 0.0).then_inc(s["const_ready"], 1)
            pool.memset(x_all[:, NB, :], 0.0).then_inc(s["const_ready"], 1)
            pool.memset(rank_rhs[:, :, :, :], 0.0).then_inc(s["const_ready"], 1)

            def rstd(n, mvr, vadd, rstdr, mv, ve, rs):
                hold(pool, mvr, n + 1)
                pool.tensor_scalar(ve[:, :], mv[:, 1:2], EPS, None, ALU.add).then_inc(s[vadd], 1)
                pool.wait_ge(s[vadd], n + 1)
                pool.tensor_tensor(rs[:, :], ve[:, :], half_neg[:, :], ALU.pow).then_inc(s[rstdr], 1)

            def body(a, b, c):
                if b is not None:
                    rstd(b, "mvr2", "vadd2", "rstdr2", mv2, ve2, rstd2)
                if a is not None:
                    rstd(a + 1, "mvr1", "vadd1", "rstdr1", mv1, ve1, rstd1)
                if b is not None:
                    rstd(b, "mvr3", "vadd3", "rstdr3", mv3, ve3, rstd3)

            pool.wait_ge(s["const_ready"], NCONST)
            rstd(0, "mvr1", "vadd1", "rstdr1", mv1, ve1, rstd1)
            pool.wait_ge(s["in_wqkv"], 16)
            for j in range(HC):
                pool.tensor_copy(w_krep[:, :, j, :], w_qkv[:, :, HEADS * HD:HEADS * HD + HD]).then_inc(s["krep_ready"], 1)
            turns(pool, body)

        @block.scalar
        def _(act):
            def copy(dst, src):
                return act.activation(dst, src, ACT.Copy)

            def body(a, b, c):
                if a is not None:
                    act.wait_ge(s["xnT_ps"], a + 1)
                    freed(act, "kv_ps", a)
                    copy(xn_t[:, :, :], P[0][:, :]).then_inc(s["xnT_ready"], 1)
                if b is not None:
                    act.wait_ge(s["fctx_ps"], b * 4 + 1)
                    freed(act, "pe_ready", b)
                    copy(fv[:, :], P[5][:, :]).then_inc(s["fctx_ready"], 1)
                    act.wait_ge(s["fctx_ps"], b * 4 + 2)
                    copy(fvx[:, :], P[5][:, :]).then_inc(s["fctx_ready"], 1)
                if a is not None:
                    act.wait_ge(s["q_ps"], a + 1)
                    freed(act, "kl_ps", a * 8)
                    act.activation(q_hi[:, :, :], P[1][:, :], ACT.Copy, scale=HD ** -0.5).then_inc(s["qhi_ready"], 1)
                    act.wait_ge(s["kv_ps"], a + 1)
                    copy(k_hi[:, :], P[0][:, 0:S]).then_inc(s["khi_ready"], 1)
                if c is not None:
                    act.wait_ge(s["hT_ps"], c + 1)
                    freed(act, "z_ps", c)
                    copy(h_t[:, :, :], P[6][:, :]).then_inc(s["hT_ready"], 1)
                    act.wait_ge(s["rq_ps"], c + 1)
                    copy(rq_t[:, :], P[6][0:RDIM, 0:S]).then_inc(s["rq_ready"], 1)
                    act.wait_ge(s["sc_ps"], c + 1)
                    copy(sc[:, :], P[6][:, 128:128 + EXPERTS]).then_inc(s["sc_ready"], 1)
                if b is not None:
                    freed(act, "po_ready", b)
                    act.wait_ge(s["fctx_ps"], b * 4 + 3)
                    copy(gv[:, :], P[5][:, :]).then_inc(s["fctx_ready"], 1)
                if c is not None:
                    act.wait_ge(s["top_c"], c * 6 + 2)
                    act.activation(esc[:, :], sc[:, :], ACT.Exp, bias=negs[:, :]).then_inc(s["esc_ready"], 1)
                if b is not None:
                    act.wait_ge(s["fctx_ps"], b * 4 + 4)
                    copy(gvx[:, :], P[5][:, :]).then_inc(s["fctx_ready"], 1)
                    act.wait_ge(s["corr_ps"], b + 1)
                    freed(act, "wtap_step", b * 3)
                    copy(corr[:, :, :], P[4][:, :]).then_inc(s["corr_ready"], 1)
                if c is not None:
                    act.wait_ge(s["zgT_ps"], c + 1)
                    copy(zg_t[:, :, :], P[6][:, :]).then_inc(s["zgT_ready"], 1)
                if b is not None:
                    act.wait_ge(s["top_a"], b * 5 + 5)
                    act.wait_ge(s["corr_ready"], b + 1)
                    for n in range(NC):
                        act.activation(ecorr[:, n, :], corr[:, n, :], ACT.Exp, bias=negtop[:, n:n + 1]).then_inc(s["ecorr_ready"], 1)
                for n, j in enumerate(JORDER):
                    if a is not None:
                        if n == 0:
                            freed(act, "pv_ps", a)
                        act.wait_ge(s["kl_ps"], a * 8 + n + 1)
                        act.activation(probs[:, j, :], P[n % 2][:, :], ACT.Exp).then_inc(s["exp_ready"], 1)
                    if b is not None and n == WT_AT:
                        act.wait_ge(s["wT_ps"], b + 1)
                        copy(wtap_t[:, :], P[4][:, :]).then_inc(s["wT_ready"], 1)

            turns(act, body)

        @block.vector
        def _(dve):
            def moments(n, src, stats, mv, stat, mvr):
                dve.bn_stats(stats[:, :], src).then_inc(s[stat], 1)
                hold(dve, stat, n + 1)
                dve.bn_aggr(mv[:, :], stats[:, :]).then_inc(s[mvr], 1)

            def normalize(n, dst, src, mv, rs, rstdr, ready):
                dve.wait_ge(s[rstdr], n + 1)
                dve.tensor_scalar(dst, src, mv[:, 0:1], rs[:, 0:1], ALU.subtract, ALU.mult).then_inc(s[ready], 1)

            def row_max(a, n):
                dve.wait_ge(s["ql_ps"], a * 8 + n + 1)
                dve.tensor_reduce(rowmax[:, 4 * n:4 * n + 4], P[n % 2][:, :].rearrange("p (j k) -> p j k", k=S), AX.X, ALU.max).then_inc(s["ql_max"], 1)

            def router(c):
                hold(dve, "sc_ready", c + 1)
                dve.max(st8a[:, :], sc[:, :]).then_inc(s["top_c"], 1)
                dve.wait_ge(s["top_c"], c * 6 + 1)
                dve.tensor_scalar(negs[:, :], st8a[:, 0:1], -1.0, None, ALU.mult).then_inc(s["top_c"], 1)
                dve.match_replace(sc2[:, :], st8a[:, :], sc[:, :], LOW).then_inc(s["top_c"], 1)
                hold(dve, "top_c", c * 6 + 3)
                dve.max(st8b[:, :], sc2[:, :]).then_inc(s["top_c"], 1)
                hold(dve, "top_c", c * 6 + 4)
                dve.match_replace(sc3[:, :], st8b[:, :], sc2[:, :], LOW).then_inc(s["top_c"], 1)
                dve.wait_ge(s["top_c"], c * 6 + 5)
                dve.wait_ge(s["esc_ready"], c + 1)
                dve.scalar_tensor_tensor(out=gate[:, :], in0=sc3[:, :], scalar=PICKED, in1=esc[:, :], op0=ALU.is_lt,
                                         op1=ALU.mult).then_inc(s["top_c"], 1)
                dve.wait_ge(s["top_c"], c * 6 + 6)
                dve.tensor_reduce(gsum[:, :], gate[:, :], AX.X, ALU.add).then_inc(s["gate_step"], 1)
                dve.wait_ge(s["gate_step"], c * 3 + 1)
                dve.reciprocal(grec[:, :], gsum[:, :]).then_inc(s["gate_step"], 1)
                dve.wait_ge(s["gate_step"], c * 3 + 2)
                dve.tensor_scalar(gate2[:, :], gate[:, :], grec[:, :], SCALING, ALU.mult, ALU.mult).then_inc(s["gate_step"], 1)
                dve.wait_ge(s["gate_step"], c * 3 + 3)
                dve.wait_ge(s["z_ps"], c + 1)
                dve.tensor_tensor(zg[:, :].rearrange("p (e r) -> p e r", r=RANK), P[7][:, :].rearrange("p (e r) -> p e r", r=RANK),
                                  gate2[:, :].rearrange("p (e o) -> p e o", o=1).broadcast_to([128, EXPERTS, RANK]),
                                  ALU.mult).then_inc(s["zg_ready"], 1)

            def delays(b):
                hold(dve, "corr_ready", b + 1)
                for n in range(NC):
                    dve.max(top8[:, n, :], corr[:, n, :]).then_inc(s["top_a"], 1)
                dve.wait_ge(s["top_a"], b * 5 + 4)
                dve.tensor_scalar(negtop[:, :], top8[:, :, 0], -1.0, None, ALU.mult).then_inc(s["top_a"], 1)
                for n in range(NC):
                    dve.match_replace(corr2[:, n, :], top8[:, n, :], corr[:, n, :], LOW).then_inc(s["top_b"], 1)
                for n in range(NC):
                    hold(dve, "top_b", b * 13 + n + 1)
                    dve.max(next8[:, n, :], corr2[:, n, :]).then_inc(s["top_b"], 1)
                dve.wait_ge(s["top_b"], b * 13 + 8)
                dve.tensor_copy(ninth[:, :, 0], next8[:, :, 0]).then_inc(s["top_b"], 1)
                hold(dve, "top_b", b * 13 + 9)
                for n in range(NC):
                    dve.match_replace(corr3[:, n, :], ninth[:, n, :], corr2[:, n, :], LOW).then_inc(s["top_b"], 1)
                dve.wait_ge(s["top_b"], b * 13 + 13)
                dve.wait_ge(s["ecorr_ready"], b * 4 + 4)
                dve.scalar_tensor_tensor(out=wtap[:, :, :], in0=corr3[:, :, :], scalar=PICKED, in1=ecorr[:, :, :],
                                         op0=ALU.is_lt, op1=ALU.mult).then_inc(s["wtap_step"], 1)
                dve.wait_ge(s["wtap_step"], b * 3 + 1)
                dve.tensor_reduce(wsum[:, :], wtap[:, :, :], AX.X, ALU.add).then_inc(s["wtap_step"], 1)
                dve.wait_ge(s["wtap_step"], b * 3 + 2)
                dve.reciprocal(wrec[:, :], wsum[:, :]).then_inc(s["wtap_step"], 1)
                dve.wait_ge(s["wtap_step"], b * 3 + 3)
                dve.tensor_tensor(wtap[:, :, :], wtap[:, :, :], wrec[:, :].rearrange("p (n o) -> p n o", o=1).broadcast_to([128, NC, S]),
                                  ALU.mult).then_inc(s["wtap_ready"], 1)

            def body(a, b, c):
                if b is not None:
                    dve.wait_ge(s["pv_ps"], b + 1)
                    dve.reciprocal(rsum[:, :], P[3][:, :]).then_inc(s["rsum_ready"], 1)
                    dve.wait_ge(s["rsum_ready"], b + 1)
                    dve.tensor_tensor(attn_t[:, :], P[2][:, :], rsum[:, :], ALU.mult).then_inc(s["attn_ready"], 1)
                if a is not None:
                    dve.wait_ge(s["qhi_ready"], a + 1)
                    dve.scalar_tensor_tensor(out=q_lo[:, :, :], in0=P[1][:, :].rearrange("p (c t) -> p c t", c=NC), scalar=HD ** -0.5,
                                             in1=q_hi[:, :, :].bitcast(F32), op0=ALU.mult, op1=ALU.subtract).then_inc(s["qlo_ready"], 1)
                    dve.wait_ge(s["khi_ready"], a + 1)
                    dve.tensor_tensor(k_lo[:, :], P[0][:, 0:S], k_hi[:, :].bitcast(F32), ALU.subtract).then_inc(s["klo_ready"], 1)
                    for par in range(2):
                        dve.tensor_copy(vpad[:, par, HD * par:HD * par + HD], P[0][:, S:S + HD]).then_inc(s["v_ready"], 1)
                    mask_b = bmask[:, :].rearrange("p (j o) -> p j o", o=1).broadcast_to([128, HC, S])
                    dve.tensor_tensor(kb_hi[:, :, :], k_hi[:, :].bitcast(F32).rearrange("p (o t) -> p o t", o=1).broadcast_to([128, HC, S]),
                                      mask_b, ALU.mult).then_inc(s["kb_ready"], 1)
                    dve.wait_ge(s["klo_ready"], a + 1)
                    dve.tensor_tensor(kb_lo[:, :, :], k_lo[:, :].rearrange("p (o t) -> p o t", o=1).broadcast_to([128, HC, S]),
                                      mask_b, ALU.mult).then_inc(s["kb_ready"], 1)
                if b is not None:
                    dve.wait_ge(s["wo_ps"], b + 1)
                    dve.tensor_tensor(x_all[:, b, :], x_all[:, b, :], P[3][:, :], ALU.add).then_inc(s["a_done"], 1)
                    hold(dve, "a_done", b + 1)
                    moments(b, x_all[:, b, :], stats2, mv2, "stat2", "mvr2")
                if a is not None:
                    row_max(a, 0)
                    row_max(a, 1)
                if b is not None:
                    normalize(b, qn[:, :], x_all[:, b, :], mv2, rstd2, "rstdr2", "qn_ready")
                if a is not None:
                    for n in range(2, 8):
                        row_max(a, n)
                if c is not None:
                    router(c)
                if a is not None:
                    dve.wait_ge(s["maxT_ps"], a + 1)
                    freed(dve, "rank_ready", a * 32)
                    dve.tensor_scalar(nm_hi[:, :], P[2][0:HEADS, 0:S], -1.0, None, ALU.mult).then_inc(s["nmax_ready"], 1)
                    dve.wait_ge(s["nmax_ready"], a * 2 + 1)
                    dve.scalar_tensor_tensor(out=nm_lo[:, :], in0=P[2][0:HEADS, 0:S], scalar=-1.0, in1=nm_hi[:, :],
                                             op0=ALU.mult, op1=ALU.subtract).then_inc(s["nmax_ready"], 1)
                if b is not None:
                    dve.wait_ge(s["fq_ps"], b + 1)
                    dve.wait_ge(s["fctx_ready"], b * 4 + 2)
                    dve.tensor_tensor(pr1[:, :], P[4][:, :], fv[:, :], ALU.mult)
                    dve.tensor_tensor(pr2[:, :], P[4][:, :], fvx[:, :], ALU.mult).then_inc(s["pr_ready"], 1)
                if a is not None:
                    moments(a + 1, x_all[:, a + 1, :], stats1, mv1, "stat1", "mvr1")
                if b is not None:
                    delays(b)
                if a is not None:
                    dve.wait_ge(s["xnT_ps"], a + 1)
                    normalize(a + 1, xn[:, :], x_all[:, a + 1, :], mv1, rstd1, "rstdr1", "xn_ready")
                if c is not None:
                    dve.wait_ge(s["ffn_ps"], c + 1)
                    dve.tensor_tensor(x_all[:, c, :], x_all[:, c, :], P[7][:, :], ALU.add).then_inc(s["c_done"], 1)
                if b is not None:
                    dve.wait_ge(s["fw_ps"], b + 1)
                    dve.tensor_tensor(pe1[:, :], P[4][:, :], fv[:, :], ALU.mult)
                    dve.tensor_tensor(pe2[:, :], P[4][:, :], fvx[:, :], ALU.mult).then_inc(s["pe_ready"], 1)
                    dve.wait_ge(s["fwo_ps"], b + 1)
                    dve.wait_ge(s["fctx_ready"], b * 4 + 4)
                    dve.tensor_tensor(po1[:, :], P[5][:, :], gv[:, :], ALU.mult)
                    dve.tensor_tensor(po2[:, :], P[5][:, :], gvx[:, :], ALU.mult).then_inc(s["po_ready"], 1)
                    dve.wait_ge(s["inv_ps"], b + 1)
                    dve.tensor_tensor(x_all[:, b, :], x_all[:, b, :], P[4][:, :], ALU.add).then_inc(s["b_done"], 1)
                    hold(dve, "b_done", b + 1)
                    moments(b, x_all[:, b, :], stats3, mv3, "stat3", "mvr3")
                    freed(dve, "hT_ps", b)
                    normalize(b, hn[:, :], x_all[:, b, :], mv3, rstd3, "rstdr3", "hn_ready")

            dve.wait_ge(s["in_x0"], 16)
            moments(0, x_all[:, 0, :], stats1, mv1, "stat1", "mvr1")
            normalize(0, xn[:, :], x_all[:, 0, :], mv1, rstd1, "rstdr1", "xn_ready")
            dve.wait_ge(s["const_ready"], NCONST)
            dve.wait_ge(s["in_small"], 16 * 2)
            dve.wait_ge(s["in_x"], 16)
            turns(dve, body)

        @block.tensor
        def _(pe):
            ident = mat[:, IDENT, :]

            def transposes(bank, src, signal):
                for n in range(NC):
                    last = pe.transpose(P[bank][:, n * 128:(n + 1) * 128], src[:, n * 128:(n + 1) * 128], ident)
                last.then_inc(s[signal], 1)

            def context(b, slot, n):
                if n:
                    pe.wait_ge(s["fctx_ready"], b * 4 + n)
                else:
                    freed(pe, "po_ready", b)
                pe.matmul(P[5][:, :], mat[:, slot, :], ctx_all[:, b, :], start=True, stop=True).then_inc(s["fctx_ps"], 1)

            def scores_by_query(a, n):
                if n == 0:
                    pe.wait_ge(s["kb_ready"], a * 2 + 1)
                    pe.wait_ge(s["qlo_ready"], a + 1)
                    pe.wait_ge(s["v_ready"], a * 2 + 2)
                if n >= 2:
                    pe.wait_ge(s["ql_max"], a * 8 + n - 1)
                ch, hf = n // 2, n % 2
                pe.matmul(P[n % 2][:, :], q_hi[:, ch, :], kb_hi[:, 4 * hf:4 * hf + 4, :], start=True, stop=False)
                pe.matmul(P[n % 2][:, :], idb[:, :], tab[:, ch, 4 * hf:4 * hf + 4, :], start=False, stop=True).then_inc(s["ql_ps"], 1)

            def scores_by_key(a, n):
                j = JORDER[n]
                if n == 0:
                    pe.wait_ge(s["kb_ready"], a * 2 + 2)
                    pe.wait_ge(s["rank_ready"], a * 32 + 32)
                if n >= 2:
                    pe.wait_ge(s["exp_ready"], a * 8 + n - 1)
                pe.matmul(P[n % 2][:, :], kb_hi[:, j, :], q_hi[:, :, :], start=True, stop=False)
                pe.matmul(P[n % 2][:, :], kb_lo[:, j, :], q_hi[:, :, :], start=False, stop=False)
                pe.matmul(P[n % 2][:, :], kb_hi[:, j, :], q_lo[:, :, :], start=False, stop=False)
                pe.matmul(P[n % 2][:, :], maskt[:, :], idb[:, :].rearrange("p (o t) -> p o t", o=1).broadcast_to([128, NC, S]),
                          start=False, stop=False)
                pe.matmul(P[n % 2][:, :], rank_lhs[:, :], rank_rhs[:, :, j, :], start=False, stop=True).then_inc(s["kl_ps"], 1)

            def body(a, b, c):
                first = isinstance(a, int) and a == 0
                if a is not None:
                    pe.wait_ge(s["xn_ready"], a + 1)
                    freed(pe, "exp_ready", a * 8)
                    transposes(0, xn[:, :], "xnT_ps")
                if isinstance(b, int) and b == 0:
                    pe.wait_ge(s["in_mat"], 16)
                    pe.wait_ge(s["in_ctx0"], 16)
                    pe.wait_ge(s["in_wo"], 16)
                if isinstance(b, int) and b == 1:
                    pe.wait_ge(s["in_ctx"], 16)
                if b is not None:
                    context(b, FV, 0)
                    context(b, FVX, 1)
                if a is not None:
                    if first:
                        pe.wait_ge(s["in_wqkv"], 16)
                    pe.wait_ge(s["xnT_ready"], a + 1)
                    for n in range(NC):
                        for k in range(NC):
                            last = pe.matmul(P[1][:, n * S:(n + 1) * S], w_qkv[:, k, n * 128:(n + 1) * 128], xn_t[:, k, :],
                                             start=(k == 0), stop=(k == NC - 1))
                    last.then_inc(s["q_ps"], 1)
                    if first:
                        pe.wait_ge(s["krep_ready"], HC)
                    for k in range(NC):
                        pe.matmul(P[0][:, 0:S], w_krep[:, k, :, :], xn_t[:, k, :], start=(k == 0), stop=(k == NC - 1))
                    for k in range(NC):
                        last = pe.matmul(P[0][:, S:S + HD], xn_t[:, k, :], w_qkv[:, k, HEADS * HD + HD:], start=(k == 0), stop=(k == NC - 1))
                    last.then_inc(s["kv_ps"], 1)
                if b is not None:
                    pe.wait_ge(s["attn_ready"], b + 1)
                    for k in range(NC):
                        last = pe.matmul(P[3][:, :], attn_t[:, k * 128:(k + 1) * 128], w_o[:, k, :], start=(k == 0), stop=(k == NC - 1))
                    last.then_inc(s["wo_ps"], 1)
                if c is not None:
                    if isinstance(c, int) and c == 0:
                        pe.wait_ge(s["in_wr"], 32)
                        pe.wait_ge(s["in_wa"], 16)
                        pe.wait_ge(s["in_wb"], 16)
                    pe.wait_ge(s["hn_ready"], c + 1)
                    freed(pe, "zgT_ready", c)
                    transposes(6, hn[:, :], "hT_ps")
                if first:
                    pe.wait_ge(s["in_small"], 16 * 2)
                    pe.wait_ge(s["in_tab"], 16)
                if a is not None:
                    scores_by_query(a, 0)
                    scores_by_query(a, 1)
                if c is not None:
                    pe.wait_ge(s["hT_ready"], c + 1)
                    for k in range(NC):
                        last = pe.matmul(P[6][0:RDIM, 0:S], w_rq[:, k, :], h_t[:, k, :], start=(k == 0), stop=(k == NC - 1))
                    last.then_inc(s["rq_ps"], 1)
                    freed(pe, "c_done", c)
                if a is not None:
                    scores_by_query(a, 2)
                for k in range(NC):
                    if c is not None:
                        last = pe.matmul(P[7][:, :], h_t[:, k, :], w_a[:, k, :], start=(k == 0), stop=(k == NC - 1))
                        if k == NC - 1:
                            last.then_inc(s["z_ps"], 1)
                        if k == 1:
                            pe.wait_ge(s["rq_ready"], c + 1)
                            pe.matmul(P[6][:, 128:128 + EXPERTS], rq_t[:, :], w_keys[:, :], start=True, stop=True).then_inc(s["sc_ps"], 1)
                    if a is not None:
                        scores_by_query(a, 3 + k)
                if a is not None:
                    scores_by_query(a, 7)
                if b is not None:
                    context(b, GV, 2)
                    pe.wait_ge(s["qn_ready"], b + 1)
                    freed(pe, "b_done", b)
                    pe.matmul(P[4][:, :], mat[:, FWD, :], qn[:, :], start=True, stop=True).then_inc(s["fq_ps"], 1)
                if a is not None:
                    if b is not None:
                        pe.wait_ge(s["attn_ready"], b + 1)
                    pe.wait_ge(s["ql_max"], a * 8 + 8)
                    pe.transpose(P[2][0:HEADS, 0:S], rowmax[:, :], ident).then_inc(s["maxT_ps"], 1)
                if b is not None:
                    context(b, GVX, 3)
                    pe.wait_ge(s["pr_ready"], b + 1)
                    for n in range(NC):
                        ch = slice(n * 128, (n + 1) * 128)
                        pe.matmul(P[4][:, ch], pr1[:, ch], mat[:, CR1, :], start=True, stop=False)
                        last = pe.matmul(P[4][:, ch], pr2[:, ch], mat[:, CR2, :], start=False, stop=True)
                    last.then_inc(s["corr_ps"], 1)
                if c is not None:
                    pe.wait_ge(s["zg_ready"], c + 1)
                    transposes(6, zg[:, :], "zgT_ps")
                    pe.wait_ge(s["zgT_ready"], c + 1)
                    for k in range(NC):
                        last = pe.matmul(P[7][:, :], zg_t[:, k, :], w_b[:, k, :], start=(k == 0), stop=(k == NC - 1))
                    last.then_inc(s["ffn_ps"], 1)
                if first:
                    pe.wait_ge(s["in_rank"], 16 * 4)
                for n in range(8):
                    if a is not None:
                        scores_by_key(a, n)
                    if b is not None and n == WT_AT:
                        pe.wait_ge(s["wtap_ready"], b + 1)
                        transposes(4, wtap[:, :, :].rearrange("p n t -> p (n t)"), "wT_ps")
                    if b is not None and n == WT_AT + 1:
                        pe.wait_ge(s["wT_ready"], b + 1)
                        pe.matmul(P[4][:, :], mat[:, FWD, :], wtap_t[:, :], start=True, stop=True).then_inc(s["fw_ps"], 1)
                        pe.wait_ge(s["fctx_ready"], b * 4 + 4)
                        pe.matmul(P[5][:, :], mat[:, GWD, :], wtap_t[:, :], start=True, stop=True).then_inc(s["fwo_ps"], 1)
                if b is not None:
                    pe.wait_ge(s["pe_ready"], b + 1)
                    pe.matmul(P[4][:, :], mat[:, EI1, :], pe1[:, :], start=True, stop=False)
                    pe.matmul(P[4][:, :], mat[:, EI2, :], pe2[:, :], start=False, stop=False)
                    pe.wait_ge(s["po_ready"], b + 1)
                    pe.matmul(P[4][:, :], mat[:, OI1, :], po1[:, :], start=False, stop=False)
                    pe.matmul(P[4][:, :], mat[:, OI2, :], po2[:, :], start=False, stop=True).then_inc(s["inv_ps"], 1)
                if a is not None:
                    if b is not None:
                        pe.wait_ge(s["a_done"], b + 1)
                    pe.wait_ge(s["nmax_ready"], a * 2 + 2)
                    for half in range(2):
                        pe.wait_ge(s["exp_ready"], a * 8 + 4 * half + 4)
                        for bank, lhs in ((2, vpad), (3, onesp)):
                            for j in JORDER[4 * half:4 * half + 4]:
                                g = 32 * (j // 2)
                                last = pe.matmul(P[bank][g:g + 32, :], lhs[:, j % 2, :], probs[:, j, :], start=(half == 0), stop=(half == 1))
                    last.then_inc(s["pv_ps"], 1)

            pe.wait_ge(s["in_ident"], 16)
            turns(pe, body)


def _constants():
    import numpy as np
    L, hlf = S, S // 2
    t = np.arange(L)[:, None].astype(np.float64)
    f = np.arange(hlf)[None, :].astype(np.float64)
    we, wo_ = 2 * np.pi * f / L, 2 * np.pi * (f + 0.5) / L
    fwd = np.concatenate([np.cos(we * t), -np.sin(we * t)], 1)
    fwd[:, hlf] = np.cos(np.pi * t[:, 0])
    swap = np.concatenate([fwd[:, hlf:], fwd[:, :hlf]], 1)
    swap[:, 0] = 1.0
    swap[:, hlf] = 0.0
    fv = fwd.copy()
    fv[L - 1, 0] += L
    gwd = np.concatenate([np.cos(wo_ * t), -np.sin(wo_ * t)], 1)
    gv = gwd.copy()
    gv[L - 1] -= gwd.sum(0)
    gvx = np.concatenate([gv[:, hlf:], gv[:, :hlf]], 1)
    tt = t.T
    ce, se = 2 * np.cos(we.T * tt) / L, 2 * np.sin(we.T * tt) / L
    base1 = np.concatenate([ce, ce], 0)
    base1[hlf] = np.cos(np.pi * tt[0]) / L
    cr1 = base1.copy()
    cr1[0] = 0.0
    cr2 = np.concatenate([se, -se], 0)
    cr2[0] = 1.0 / L
    cr2[hlf] = 0.0
    ei1 = base1.copy()
    ei1[0] = 1.0 / L
    ei2 = np.concatenate([-se, se], 0)
    ei2[0] = 0.0
    ei2[hlf] = 0.0
    co, so = 2 * np.cos(wo_.T * tt) / L, 2 * np.sin(wo_.T * tt) / L
    oi1 = np.concatenate([co, co], 0)
    oi2 = np.concatenate([-so, so], 0)
    mats = np.stack([fwd, fv, swap, gv, gvx, gwd, cr1, cr2, ei1 / 2, ei2 / 2, oi1 / 2, oi2 / 2, np.eye(L)], 1).astype(np.float32)
    bf = mybir.dt.np(BF16)
    slopes = ((2.0 ** (-2.0 ** (-(np.log2(HEADS) - 3)))) ** np.arange(1, HEADS + 1)).astype(np.float32)
    pos = np.arange(S)
    table = slopes.reshape(1, NC, HC, 1) * pos.reshape(1, 1, 1, S).astype(np.float32)
    table = np.where(pos.reshape(1, 1, 1, S) > pos.reshape(S, 1, 1, 1), np.float32(-1e30), table).astype(bf)
    rank_l = np.zeros((128, 128), bf)
    rank_l[0:3] = pos.astype(bf)
    rank_l[3:5] = 1.0
    rank_r = np.zeros((3, NC, HC, S), bf)
    rest = slopes.copy()
    for n in range(3):
        part = rest.astype(bf)
        rank_r[n] = part.reshape(NC, HC, 1)
        rest = rest - part.astype(np.float32)
    blockmask = (np.arange(128)[:, None] // HD == np.arange(HC)[None, :]).astype(np.float32)
    ones_pad = np.zeros((128, 2, 32), np.float32)
    ones_pad[:, 0, :HD] = 1.0
    ones_pad[:, 1, HD:] = 1.0
    return {"mats": mats, "table": table, "rank_l": rank_l, "rank_r": rank_r, "blockmask": blockmask, "ones_pad": ones_pad,
            "identb": np.eye(128).astype(bf), "causal": np.where(pos[None, :] > pos[:, None], np.float32(-1e30), np.float32(0)).astype(bf)}


def kernel(x, ctx_4096, L0_attn_Wqkv, L0_attn_Wo, L0_ffn_A_w, L0_ffn_B_w, L0_ffn_Wq_w, L0_ffn_keys):
    import numpy as np
    import concourse.bacc as bacc
    from concourse.bass_utils import run_bass_kernel_spmd

    nc = bacc.Bacc("TRN2", target_bir_lowering=False, num_devices=1)
    arrays = {
        "x": x, "ctx": ctx_4096, "wqkv": L0_attn_Wqkv, "wo": L0_attn_Wo, "a_t": np.asarray(L0_ffn_A_w).T,
        "b_t": np.asarray(L0_ffn_B_w).T, "wq_t": np.asarray(L0_ffn_Wq_w).T, "keys_t": np.asarray(L0_ffn_keys).T,
        **_constants(),
    }
    arrays = {f"in_{n}": np.ascontiguousarray(v) for n, v in arrays.items()}
    args = [nc.dram_tensor(n, v.shape, mybir.dt.from_np(v.dtype), kind="ExternalInput").ap() for n, v in arrays.items()]
    out = nc.dram_tensor("out", (NB, S, D), F32, kind="ExternalOutput").ap()
    decoder_layer(nc, *args, out)
    r = run_bass_kernel_spmd(nc, [arrays], core_ids=[0])
    return r.results[0]["out"]
```

```python
from contextlib import ExitStack

import concourse.bass as bass
from concourse import mybir

F32 = mybir.dt.float32
F32R = mybir.dt.float32r
BF16 = mybir.dt.bfloat16
ALU = mybir.AluOpType
ACT = mybir.ActivationFunctionType
AX = mybir.AxisListType

NB, S, D = 8, 128, 512
NC = D // 128
HEADS, HD = 32, 16
HC = 128 // HD
EXPERTS, RANK, RDIM = 64, 8, 16
TAPS, TOPK = 9, 16
SCALING = 32.0 / TOPK
EPS = 1e-5
LOW = -3.0e38
PICKED = -1.0e38

(FWD, GV, GWD, CR1, CR2, EI1, EI2, OI1, OI2, IDENT) = range(10)
NMATS = 10
BY_QUERY = (0, 1, 2, 0, 1, 2, 0, 3)
BY_KEY = (0, 1, 6)
NCONST = 6
PAIRS = [(0, 0), (0, 1), (0, 2), (1, 0), (1, 1), (2, 0)]
QROWS = len(PAIRS) * HD
KROWS = QROWS + 5
JORDER = [0, 2, 4, 6, 1, 3, 5, 7]


def decoder_layer(nc, x, ctx_in, wqkv, wo, a_t, b_t, wq_t, keys_t, mats, pos, slope, rank_l, rank_r, blockmask, parts, ones_pad,
                  identb, causal, sum_k, sum_v, out):
    st = ExitStack()
    with st:
        def sb(name, shape, dt=F32):
            return st.enter_context(nc.sbuf_tensor(name, shape, dt))

        def pb(name, dt=F32):
            return st.enter_context(nc.psum_tensor(name, [128, 512], dt))

        def sem(name):
            return st.enter_context(nc.semaphore(name))

        x_all = sb("x_all", [128, NB + 1, D])
        ctx_raw = sb("ctx_raw", [128, D])
        ctx_last = sb("ctx_last", [1, D])
        mat = sb("mat", [128, NMATS, 128])
        w_qkv = sb("w_qkv", [128, NC, HEADS * HD + 2 * HD])
        sel_k = sb("sel_k", [128, 128])
        sel_v = sb("sel_v", [128, HD])
        stage = sb("stage", [128, NC, D])
        w_o = [sb(f"w_o{h}", [128, NC, D], F32R) for h in range(2)]
        w_a = [sb(f"w_a{h}", [128, NC, D], F32R) for h in range(2)]
        w_b = [sb(f"w_b{h}", [128, NC, D], F32R) for h in range(2)]
        mctx = [sb(f"mctx{h}", [128, 2, 128], F32R) for h in range(2)]
        ctx_h = [sb(f"ctx_h{h}", [128, D], F32R) for h in range(2)]
        w_rq = sb("w_rq", [128, NC, 32])
        w_keys = sb("w_keys", [128, EXPERTS])
        tab = sb("tab", [128, NC, HC, S], BF16)
        positions = sb("positions", [128, S])
        slopes = sb("slopes", [128, HEADS])
        rank_lhs = sb("rank_lhs", [128, 128], BF16)
        part_mask = sb("part_mask", [128, 3])
        bmask = sb("bmask", [128, HC])
        onesp = sb("onesp", [128, 2, 32])
        idb = sb("idb", [128, 128], BF16)
        maskt = sb("maskt", [128, 128], BF16)
        half_neg = sb("half_neg", [128, 1])
        stats1 = sb("stats1", [128, 6]); mv1 = sb("mv1", [128, 2]); ve1 = sb("ve1", [128, 1]); rstd1 = sb("rstd1", [128, 1])
        xn = sb("xn", [128, D])
        xn_t = sb("xn_t", [128, NC, S])
        q_hi = sb("q_hi", [128, NC, S], F32R)
        q_part = [sb(f"q_part{n}", [128, NC * S], BF16) for n in range(3)]
        q_rest = sb("q_rest", [128, NC * S])
        kv_t = sb("kv_t", [128, S])
        q_f = sb("q_f", [128, NC * S])
        k_hi = sb("k_hi", [128, S], F32R)
        k_f = sb("k_f", [128, S])
        k_part = [sb(f"k_part{n}", [128, S], BF16) for n in range(3)]
        k_rest = sb("k_rest", [128, S])
        k_rows = [sb(f"k_rows{n}", [128, S], BF16) for n in range(3)]
        k_rows01 = sb("k_rows01", [128, S], BF16)
        k_rows2r = sb("k_rows2r", [128, S], BF16)
        k_stack = sb("k_stack", [128, S], BF16)
        kb_hi = sb("kb_hi", [128, HC, S], F32R)
        q_stack = sb("q_stack", [KROWS, HC, NC, S], BF16)
        vpad = sb("vpad", [128, 2, 32])
        rowmax = sb("rowmax", [128, HC, NC])
        nm_hi = sb("nm_hi", [HEADS, S], BF16)
        nm_lo = sb("nm_lo", [HEADS, S], BF16)
        probs = sb("probs", [128, HC, NC * S])
        rsum = sb("rsum", [128, D])
        attn_h = [sb(f"attn_h{h}", [128, D], F32R) for h in range(2)]
        stats2 = sb("stats2", [128, 6]); mv2 = sb("mv2", [128, 2]); ve2 = sb("ve2", [128, 1]); rstd2 = sb("rstd2", [128, 1])
        qn = sb("qn", [128, D])
        fv = sb("fv", [128, D]); fvx = sb("fvx", [128, D]); gv = sb("gv", [128, D]); gvx = sb("gvx", [128, D])
        pr1 = sb("pr1", [128, D]); pr2 = sb("pr2", [128, D])
        corr = sb("corr", [128, NC, S]); corr2 = sb("corr2", [128, NC, S])
        top8 = sb("top8", [128, NC, 8]); next8 = sb("next8", [128, NC, 8]); ninth = sb("ninth", [128, NC, 8])
        negtop = sb("negtop", [128, NC])
        ecorr = sb("ecorr", [128, NC, S])
        wtap = sb("wtap", [128, NC, S]); wsum = sb("wsum", [128, NC]); wrec = sb("wrec", [128, NC])
        wtap_t = sb("wtap_t", [128, D])
        po1 = sb("po1", [128, D]); po2 = sb("po2", [128, D])
        stats3 = sb("stats3", [128, 6]); mv3 = sb("mv3", [128, 2]); ve3 = sb("ve3", [128, 1]); rstd3 = sb("rstd3", [128, 1])
        hn = sb("hn", [128, D])
        h_t = sb("h_t", [128, NC, S])
        h_h = [sb(f"h_h{h}", [128, NC, S], F32R) for h in range(2)]
        rq_t = sb("rq_t", [128, S])
        sc = sb("sc", [128, EXPERTS]); sc2 = sb("sc2", [128, EXPERTS]); sc3 = sb("sc3", [128, EXPERTS])
        st8a = sb("st8a", [128, 8]); st8b = sb("st8b", [128, 8]); negs = sb("negs", [128, 1])
        esc = sb("esc", [128, EXPERTS]); gate = sb("gate", [128, EXPERTS]); gsum = sb("gsum", [128, 1]); grec = sb("grec", [128, 1])
        gate2 = sb("gate2", [128, EXPERTS])
        z_f = sb("z_f", [128, D])
        zg = sb("zg", [128, D])
        zg_h = [sb(f"zg_h{h}", [128, NC, S], F32R) for h in range(2)]

        q_dram = nc.dram_tensor("q_parts", (3, 128, NC * S), BF16).ap()

        P = [pb(f"bank{i}") for i in range(8)]

        names = """held in_ident in_rank in_x0 in_x1 in_x in_ctx in_last in_mat in_wqkv in_wo in_wa in_wb in_wr in_small tab_ready
            const_ready stat1 mvr1 vadd1 rstdr1 xn_ready xnT_ps xnT_ready q_ps qhi_ready q1_ready qf_ready qrest_ready
            q2_ready q3_ready kv4_ps kv_ps kvt_ready khi_ready kf_ready kstep k1_ready krows_ready kstack_ready kb_ready
            v_ready q_sent0 q_sent1 q_sent2 q_stacked attn_f attn_hi hT_hi hT_lo zgT_hi wsplit mctx_ready ctx_hi ctx_ready
            ql_ps ql_max maxT_ps nmax_ready rank_ready kl_ps exp_ready pv_ps den_ps rsum_ready attn_ready wo_ps a_done stat2
            mvr2 vadd2 rstdr2 qn_ready fq_ps fctx_ps fv_ready gv_ready pr_ready corr_ps corr_ready top_a top_b ecorr_ready
            wtap_step wtap_ready wT_ps wT_ready fw_ps pe_ready fwo_ps po_ready inv_ps b_done stat3 mvr3 vadd3 rstdr3
            hn_ready hT_ps hT_ready z_ps zf_ready rq_ps rq_ready sc_ps sc_ready top_c esc_ready gate_step zg_ready zgT_ps
            zgT_ready ffn_ps c_done out_done""".split()
        s = {n: sem(n) for n in names}

        def hold(eng, name, value):
            eng.wait_ge(s[name], value)
            if not isinstance(value, int):
                eng.sem_inc(s["held"], 1)

        def freed(eng, name, value, alone=False):
            if not isinstance(value, int) or value > 0:
                if alone:
                    hold(eng, name, value)
                else:
                    eng.wait_ge(s[name], value)

        block = st.enter_context(nc.Block())

        def gated(eng, c, z):
            eng.wait_ge(s["gate_step"], c * 3 + 3)
            freed(eng, "zgT_ps", c)
            eng.tensor_tensor(zg[:, :].rearrange("p (e r) -> p e r", r=RANK), z[:, :].rearrange("p (e r) -> p e r", r=RANK),
                              gate2[:, :].rearrange("p (e o) -> p e o", o=1).broadcast_to([128, EXPERTS, RANK]),
                              ALU.mult).then_inc(s["zg_ready"], 1)

        def turns(eng, body):
            body(0, None, None)
            body(1, 0, None)
            body(2, 1, 0)
            with eng.Fori(3, NB) as i:
                body(i, i - 1, i - 2)
            body(None, NB - 1, NB - 2)
            body(None, None, NB - 1)

        @block.sync
        def _(sp):
            sp.dma_start(x_all[:, 0, :], x[0]).then_inc(s["in_x0"], 16)
            sp.dma_start(mat[:, IDENT, :], mats[:, IDENT, :]).then_inc(s["in_ident"], 16)
            sp.dma_start(w_qkv[:, :, :], wqkv.rearrange("(k p) n -> p k n", p=128)).then_inc(s["in_wqkv"], 16)
            for dst, src in ((maskt, causal), (positions, pos), (slopes, slope), (bmask, blockmask), (idb, identb), (sel_k, sum_k),
                             (sel_v, sum_v)):
                sp.dma_start(dst[:, :], src).then_inc(s["in_small"], 16)
            sp.dma_start(rank_lhs[:, :], rank_l).then_inc(s["in_rank"], 16)
            sp.dma_start(q_stack[QROWS:QROWS + 3, :, :, :], rank_r).then_inc(s["in_rank"], 16)
            sp.dma_start(part_mask[:, :], parts).then_inc(s["in_rank"], 16)
            sp.dma_start(onesp[:, :, :], ones_pad).then_inc(s["in_rank"], 16)
            sp.dma_start(stage[:, :, :], wo.rearrange("(k p) n -> p k n", p=128)).then_inc(s["in_wo"], 16)
            sp.dma_start(x_all[:, 1, :], x[1]).then_inc(s["in_x1"], 16)
            sp.dma_start(mat[:, 0:IDENT, :], mats[:, 0:IDENT, :]).then_inc(s["in_mat"], 16)

            def body(a, b, c):
                if a is not None:
                    freed(sp, "ctx_ready", a, alone=True)
                    sp.dma_start(ctx_raw[:, :], ctx_in[bass.ds(a, 1)].rearrange("b t d -> (b t) d")).then_inc(s["in_ctx"], 16)
                    freed(sp, "fv_ready", a * 4, alone=True)
                    sp.dma_start(ctx_last[:, :], ctx_in[bass.ds(a, 1), S - 1, :]).then_inc(s["in_last"], 16)
                    freed(sp, "q_stacked", a * 96, alone=True)

                    def send(n, ready, value):
                        hold(sp, ready, value)
                        sp.dma_start(q_dram[n], q_part[n][:, :]).then_inc(s[f"q_sent{n}"], 16)

                    def stack(n):
                        hold(sp, f"q_sent{n}", a * 16 + 16)
                        for row, (qp, _) in enumerate(PAIRS):
                            if qp == n:
                                sp.dma_start(q_stack[row * HD:(row + 1) * HD, :, :, :], q_dram[n].rearrange("(j d) n -> d j n", d=HD)
                                             ).then_inc(s["q_stacked"], 16)

                    send(0, "q1_ready", a * 2 + 2)
                    send(1, "q2_ready", a + 1)
                    freed(sp, "kl_ps", a * 8, alone=True)
                    stack(0)
                    send(2, "q3_ready", a + 1)
                    stack(1)
                    stack(2)
                    hold(sp, "nmax_ready", a * 2 + 1)
                    sp.dma_start(q_stack[QROWS + 3:QROWS + 4, :, :, :], nm_hi[:, :]).then_inc(s["rank_ready"], 16)
                    hold(sp, "nmax_ready", a * 2 + 2)
                    sp.dma_start(q_stack[QROWS + 4:QROWS + 5, :, :, :], nm_lo[:, :]).then_inc(s["rank_ready"], 16)
                    if isinstance(a, int) and a == 0:
                        sp.dma_start(x_all[:, 2:NB, :], x[2:NB].rearrange("b t d -> t b d")).then_inc(s["in_x"], 16)
                        sp.wait_ge(s["const_ready"], NCONST)
                        sp.dma_start(w_rq[:, :, 0:RDIM], wq_t.rearrange("(k p) n -> p k n", p=128)).then_inc(s["in_wr"], 16)
                        for k in range(NC):
                            sp.dma_start(w_keys[32 * k:32 * k + RDIM, :], keys_t).then_inc(s["in_wr"], 16)
                        sp.wait_ge(s["wsplit"], 2)
                        sp.dma_start(stage[:, :, :], a_t.rearrange("(k p) n -> p k n", p=128)).then_inc(s["in_wa"], 16)
                    if isinstance(a, int) and a == 1:
                        sp.wait_ge(s["wsplit"], 4)
                        sp.dma_start(stage[:, :, :], b_t.rearrange("(k p) n -> p k n", p=128)).then_inc(s["in_wb"], 16)
                if c is not None:
                    hold(sp, "c_done", c + 1)
                    sp.dma_start(out[bass.ds(c, 1)].rearrange("b t d -> (b t) d"), x_all[:, c, :]).then_inc(s["out_done"], 16)

            turns(sp, body)
            sp.wait_ge(s["out_done"], 16 * NB)

        @block.gpsimd
        def _(pool):
            pool.memset(half_neg[:, :], -0.5).then_inc(s["const_ready"], 1)
            pool.memset(ninth[:, :, :], LOW).then_inc(s["const_ready"], 1)
            pool.memset(w_rq[:, :, :], 0.0).then_inc(s["const_ready"], 1)
            pool.memset(w_keys[:, :], 0.0).then_inc(s["const_ready"], 1)
            pool.memset(vpad[:, :, :], 0.0).then_inc(s["const_ready"], 1)
            pool.memset(x_all[:, NB, :], 0.0).then_inc(s["const_ready"], 1)

            def rstd(n, mvr, vadd, rstdr, mv, ve, rs):
                hold(pool, mvr, n + 1)
                pool.tensor_scalar(ve[:, :], mv[:, 1:2], EPS, None, ALU.add).then_inc(s[vadd], 1)
                pool.wait_ge(s[vadd], n + 1)
                pool.tensor_tensor(rs[:, :], ve[:, :], half_neg[:, :], ALU.pow).then_inc(s[rstdr], 1)

            def split_context(n):
                freed(pool, "fctx_ps", n * 2, alone=True)
                hold(pool, "in_ctx", n * 16 + 16)
                pool.tensor_copy(ctx_h[0][:, :], ctx_raw[:, :]).then_inc(s["ctx_hi"], 1)
                pool.wait_ge(s["ctx_hi"], n + 1)
                pool.tensor_tensor(ctx_h[1][:, :], ctx_raw[:, :], ctx_h[0][:, :].bitcast(F32), ALU.subtract).then_inc(s["ctx_ready"], 1)

            def body(a, b, c):
                if a is not None:
                    pool.wait_ge(s["khi_ready"], a + 1)
                    freed(pool, "ql_ps", a * 8)
                    pool.tensor_tensor(kb_hi[:, :, :], k_hi[:, :].bitcast(F32).rearrange("p (o t) -> p o t", o=1).broadcast_to([128, HC, S]),
                                       bmask[:, :].rearrange("p (j o) -> p j o", o=1).broadcast_to([128, HC, S]),
                                       ALU.mult).then_inc(s["kb_ready"], 1)
                if a is not None and c is not None:
                    pool.wait_ge(s["hT_ready"], c + 1)
                    pool.wait_ge(s["hT_hi"], c + 1)
                    freed(pool, "z_ps", c, alone=True)
                    pool.tensor_tensor(h_h[1][:, :, :], h_t[:, :, :], h_h[0][:, :, :].bitcast(F32),
                                       ALU.subtract).then_inc(s["hT_lo"], 1)
                if a is not None:
                    pool.wait_ge(s["q1_ready"], a * 2 + 2)
                    pool.wait_ge(s["qf_ready"], a * 2 + 2)
                    freed(pool, "q3_ready", a)
                    pool.tensor_tensor(q_rest[:, :], q_f[:, :], q_part[0][:, :], ALU.subtract).then_inc(s["qrest_ready"], 1)
                    hold(pool, "qrest_ready", a + 1)
                    freed(pool, "q_sent1", a * 16, alone=True)
                    pool.tensor_copy(q_part[1][:, :], q_rest[:, :]).then_inc(s["q2_ready"], 1)
                    pool.wait_ge(s["q2_ready"], a + 1)
                    freed(pool, "q_sent2", a * 16)
                    pool.tensor_tensor(q_part[2][:, :], q_rest[:, :], q_part[1][:, :], ALU.subtract).then_inc(s["q3_ready"], 1)
                if b is not None:
                    rstd(b, "mvr2", "vadd2", "rstdr2", mv2, ve2, rstd2)
                if a is not None and c is not None:
                    pool.wait_ge(s["zf_ready"], c + 1)
                    gated(pool, c, z_f)
                if a is not None:
                    pool.wait_ge(s["k1_ready"], a + 1)
                    pool.tensor_tensor(k_rest[:, :], k_f[:, :], k_part[0][:, :], ALU.subtract).then_inc(s["kstep"], 1)
                    hold(pool, "kstep", a * 7 + 1)
                    pool.tensor_copy(k_part[1][:, :], k_rest[:, :]).then_inc(s["kstep"], 1)
                    pool.wait_ge(s["kstep"], a * 7 + 2)
                    pool.tensor_tensor(k_part[2][:, :], k_rest[:, :], k_part[1][:, :], ALU.subtract).then_inc(s["kstep"], 1)
                    pool.wait_ge(s["kstep"], a * 7 + 3)
                    for n in (1, 2):
                        pool.tensor_tensor(k_rows[n][:, :], k_part[n][:, :], part_mask[:, n:n + 1].broadcast_to([128, S]),
                                           ALU.mult).then_inc(s["kstep"], 1)
                    pool.wait_ge(s["kstep"], a * 7 + 5)
                    pool.wait_ge(s["krows_ready"], a + 1)
                    pool.tensor_tensor(k_rows01[:, :], k_rows[0][:, :], k_rows[1][:, :], ALU.add).then_inc(s["kstep"], 1)
                    pool.tensor_tensor(k_rows2r[:, :], k_rows[2][:, :], rank_lhs[:, :], ALU.add).then_inc(s["kstep"], 1)
                    pool.wait_ge(s["kstep"], a * 7 + 7)
                    freed(pool, "kl_ps", a * 8)
                    pool.tensor_tensor(k_stack[:, :], k_rows01[:, :], k_rows2r[:, :], ALU.add).then_inc(s["kstack_ready"], 1)
                if isinstance(a, int) and a == 1:
                    pool.wait_ge(s["wsplit"], 3)
                    pool.tensor_tensor(w_a[1][:, :, :], stage[:, :, :], w_a[0][:, :, :].bitcast(F32), ALU.subtract).then_inc(s["wsplit"], 1)
                if a is not None:
                    rstd(a + 1, "mvr1", "vadd1", "rstdr1", mv1, ve1, rstd1)
                    split_context(a)
                if isinstance(a, int) and a == 0:
                    pool.wait_ge(s["mctx_ready"], 1)
                    pool.tensor_tensor(mctx[1][:, :, :], mat[:, FWD:FWD + 2, :], mctx[0][:, :, :].bitcast(F32), ALU.subtract).then_inc(s["mctx_ready"], 1)
                    pool.wait_ge(s["wsplit"], 1)
                    pool.tensor_tensor(w_o[1][:, :, :], stage[:, :, :], w_o[0][:, :, :].bitcast(F32), ALU.subtract).then_inc(s["wsplit"], 1)
                if b is not None:
                    rstd(b, "mvr3", "vadd3", "rstdr3", mv3, ve3, rstd3)

            pool.wait_ge(s["const_ready"], NCONST)
            rstd(0, "mvr1", "vadd1", "rstdr1", mv1, ve1, rstd1)
            pool.wait_ge(s["in_small"], 16 * 7)
            pool.wait_ge(s["in_rank"], 16 * 4)
            turns(pool, body)

        @block.scalar
        def _(act):
            def copy(dst, src):
                return act.activation(dst, src, ACT.Copy)

            def body(a, b, c):
                if a is not None:
                    act.wait_ge(s["xnT_ps"], a + 1)
                    freed(act, "kv_ps", a)
                    copy(xn_t[:, :, :], P[0][:, :]).then_inc(s["xnT_ready"], 1)
                    act.wait_ge(s["kv4_ps"], a + 1)
                    freed(act, "v_ready", a * 2)
                    copy(kv_t[:, :], P[0][:, 0:S]).then_inc(s["kvt_ready"], 1)
                    act.wait_ge(s["kv_ps"], a + 1)
                    copy(k_hi[:, :], P[0][:, S:2 * S]).then_inc(s["khi_ready"], 1)
                    copy(k_f[:, :], P[0][:, S:2 * S]).then_inc(s["kf_ready"], 1)
                if b is not None:
                    act.wait_ge(s["fctx_ps"], b * 2 + 1)
                    freed(act, "pe_ready", b)
                    copy(fv[:, :], P[5][:, :]).then_inc(s["fv_ready"], 1)
                    act.wait_ge(s["attn_f"], b + 1)
                    copy(attn_h[0][:, :], rsum[:, :]).then_inc(s["attn_hi"], 1)
                def q_half(half):
                    ch = slice(half * 2 * S, half * 2 * S + 2 * S)
                    act.wait_ge(s["q_ps"], a * 2 + half + 1)
                    act.activation(q_hi[:, 2 * half:2 * half + 2, :], P[1 + half][:, 0:2 * S], ACT.Copy, scale=HD ** -0.5).then_inc(s["qhi_ready"], 1)
                    if half == 0:
                        freed(act, "qrest_ready", a)
                        freed(act, "q_sent0", a * 16)
                    act.activation(q_f[:, ch], P[1 + half][:, 0:2 * S], ACT.Copy, scale=HD ** -0.5).then_inc(s["qf_ready"], 1)
                    act.activation(q_part[0][:, ch], P[1 + half][:, 0:2 * S], ACT.Copy, scale=HD ** -0.5).then_inc(s["q1_ready"], 1)

                if c is not None:
                    act.wait_ge(s["hT_ps"], c + 1)
                    freed(act, "z_ps", c)
                    copy(h_t[:, :, :], P[6][:, :]).then_inc(s["hT_ready"], 1)
                    copy(h_h[0][:, :, :], P[6][:, :]).then_inc(s["hT_hi"], 1)
                if a is not None:
                    q_half(0)
                if c is not None:
                    act.wait_ge(s["rq_ps"], c + 1)
                    copy(rq_t[:, :], P[7][:, 0:S]).then_inc(s["rq_ready"], 1)
                if a is not None:
                    q_half(1)
                if c is not None:
                    act.wait_ge(s["sc_ps"], c + 1)
                    copy(sc[:, :], P[6][:, 128:128 + EXPERTS]).then_inc(s["sc_ready"], 1)
                    act.wait_ge(s["top_c"], c * 6 + 2)
                    act.activation(esc[:, :], sc[:, :], ACT.Exp, bias=negs[:, :]).then_inc(s["esc_ready"], 1)
                if b is not None:
                    copy(fvx[0:64, :], P[5][64:128, :]).then_inc(s["fv_ready"], 1)
                    copy(fvx[64:128, :], P[5][0:64, :]).then_inc(s["fv_ready"], 1)
                    act.wait_ge(s["in_last"], b * 16 + 16)
                    act.wait_ge(s["fv_ready"], b * 4 + 3)
                    copy(fvx[0:1, :], ctx_last[:, :]).then_inc(s["fv_ready"], 1)
                if a is not None:
                    act.wait_ge(s["kf_ready"], a + 1)
                    if isinstance(a, int) and a == 0:
                        act.wait_ge(s["in_rank"], 16 * 4)
                    freed(act, "kstack_ready", a)
                    copy(k_part[0][:, :], k_f[:, :]).then_inc(s["k1_ready"], 1)
                    act.activation(k_rows[0][:, :], k_f[:, :], ACT.Copy, scale=part_mask[:, 0:1]).then_inc(s["krows_ready"], 1)
                if isinstance(a, int) and a == 0:
                    act.wait_ge(s["in_wo"], 16)
                    copy(w_o[0][:, :, :], stage[:, :, :]).then_inc(s["wsplit"], 1)
                    act.wait_ge(s["in_mat"], 16)
                    copy(mctx[0][:, :, :], mat[:, FWD:FWD + 2, :]).then_inc(s["mctx_ready"], 1)
                if isinstance(a, int) and a == 1:
                    act.wait_ge(s["in_wa"], 16)
                    copy(w_a[0][:, :, :], stage[:, :, :]).then_inc(s["wsplit"], 1)
                if a is not None and c is not None:
                    act.wait_ge(s["z_ps"], c + 1)
                    freed(act, "zg_ready", c)
                    copy(z_f[:, :], P[7][:, :]).then_inc(s["zf_ready"], 1)
                if b is not None:
                    freed(act, "po_ready", b)
                    act.wait_ge(s["fctx_ps"], b * 2 + 2)
                    copy(gv[:, :], P[5][:, :]).then_inc(s["gv_ready"], 1)
                if c is not None:
                    act.wait_ge(s["zgT_ps"], c + 1)
                    copy(zg_h[0][:, :, :], P[6][:, :]).then_inc(s["zgT_hi"], 1)
                if b is not None:
                    copy(gvx[0:64, :], P[5][64:128, :]).then_inc(s["gv_ready"], 1)
                    copy(gvx[64:128, :], P[5][0:64, :]).then_inc(s["gv_ready"], 1)
                    act.wait_ge(s["corr_ps"], b + 1)
                    freed(act, "wtap_step", b * 3)
                    copy(corr[:, :, :], P[4][:, :]).then_inc(s["corr_ready"], 1)
                    act.wait_ge(s["top_a"], b * 5 + 5)
                    act.wait_ge(s["corr_ready"], b + 1)
                    for n in range(NC):
                        act.activation(ecorr[:, n, :], corr[:, n, :], ACT.Exp, bias=negtop[:, n:n + 1]).then_inc(s["ecorr_ready"], 1)
                for n, j in enumerate(JORDER):
                    if a is not None:
                        if n == 0:
                            freed(act, "pv_ps", a)
                        act.wait_ge(s["kl_ps"], a * 8 + n + 1)
                        act.activation(probs[:, j, :], P[BY_KEY[n % 3]][:, :], ACT.Exp).then_inc(s["exp_ready"], 1)
                if b is not None:
                    act.wait_ge(s["wT_ps"], b + 1)
                    copy(wtap_t[:, :], P[4][:, :]).then_inc(s["wT_ready"], 1)
                if isinstance(a, int) and a == 1:
                    act.wait_ge(s["in_wb"], 16)
                    copy(w_b[0][:, :, :], stage[:, :, :]).then_inc(s["wsplit"], 1)

            turns(act, body)

        @block.vector
        def _(dve):
            def moments(n, src, stats, mv, stat, mvr):
                dve.bn_stats(stats[:, :], src).then_inc(s[stat], 1)
                hold(dve, stat, n + 1)
                dve.bn_aggr(mv[:, :], stats[:, :]).then_inc(s[mvr], 1)

            def normalize(n, dst, src, mv, rs, rstdr, ready):
                dve.wait_ge(s[rstdr], n + 1)
                dve.tensor_scalar(dst, src, mv[:, 0:1], rs[:, 0:1], ALU.subtract, ALU.mult).then_inc(s[ready], 1)

            def row_max(a, n):
                dve.wait_ge(s["ql_ps"], a * 8 + n + 1)
                dve.tensor_reduce(rowmax[:, 4 * (n % 2):4 * (n % 2) + 4, n // 2], P[BY_QUERY[n]][:, :].rearrange("p (j k) -> p j k", k=S), AX.X, ALU.max).then_inc(s["ql_max"], 1)

            def router(c):
                hold(dve, "sc_ready", c + 1)
                dve.max(st8a[:, :], sc[:, :]).then_inc(s["top_c"], 1)
                dve.wait_ge(s["top_c"], c * 6 + 1)
                dve.tensor_scalar(negs[:, :], st8a[:, 0:1], -1.0, None, ALU.mult).then_inc(s["top_c"], 1)
                dve.match_replace(sc2[:, :], st8a[:, :], sc[:, :], LOW).then_inc(s["top_c"], 1)
                hold(dve, "top_c", c * 6 + 3)
                dve.max(st8b[:, :], sc2[:, :]).then_inc(s["top_c"], 1)

            def router_gates(c):
                hold(dve, "top_c", c * 6 + 4)
                dve.match_replace(sc3[:, :], st8b[:, :], sc2[:, :], LOW).then_inc(s["top_c"], 1)

            def router_picked(c):
                dve.wait_ge(s["top_c"], c * 6 + 5)
                dve.wait_ge(s["esc_ready"], c + 1)
                dve.scalar_tensor_tensor(out=gate[:, :], in0=sc3[:, :], scalar=PICKED, in1=esc[:, :], op0=ALU.is_lt,
                                         op1=ALU.mult).then_inc(s["top_c"], 1)

            def router_sum(c):
                dve.wait_ge(s["top_c"], c * 6 + 6)
                dve.tensor_reduce(gsum[:, :], gate[:, :], AX.X, ALU.add).then_inc(s["gate_step"], 1)

            def router_scale(c):
                dve.wait_ge(s["gate_step"], c * 3 + 1)
                dve.reciprocal(grec[:, :], gsum[:, :]).then_inc(s["gate_step"], 1)
                dve.wait_ge(s["gate_step"], c * 3 + 2)
                freed(dve, "zg_ready", c)
                dve.tensor_scalar(gate2[:, :], gate[:, :], grec[:, :], SCALING, ALU.mult, ALU.mult).then_inc(s["gate_step"], 1)

            def delays(b):
                hold(dve, "corr_ready", b + 1)
                for n in range(NC):
                    dve.max(top8[:, n, :], corr[:, n, :]).then_inc(s["top_a"], 1)
                dve.wait_ge(s["top_a"], b * 5 + 4)
                dve.tensor_scalar(negtop[:, :], top8[:, :, 0], -1.0, None, ALU.mult).then_inc(s["top_a"], 1)
                for n in range(NC):
                    dve.match_replace(corr2[:, n, :], top8[:, n, :], corr[:, n, :], LOW).then_inc(s["top_b"], 1)
                for n in range(NC):
                    hold(dve, "top_b", b * 13 + n + 1)
                    dve.max(next8[:, n, :], corr2[:, n, :]).then_inc(s["top_b"], 1)
                dve.wait_ge(s["top_b"], b * 13 + 8)
                dve.tensor_copy(ninth[:, :, 0], next8[:, :, 0]).then_inc(s["top_b"], 1)
                hold(dve, "top_b", b * 13 + 9)
                for n in range(NC):
                    dve.match_replace(corr2[:, n, :], ninth[:, n, :], corr2[:, n, :], LOW).then_inc(s["top_b"], 1)
                dve.wait_ge(s["top_b"], b * 13 + 13)
                dve.wait_ge(s["ecorr_ready"], b * 4 + 4)
                dve.scalar_tensor_tensor(out=wtap[:, :, :], in0=corr2[:, :, :], scalar=PICKED, in1=ecorr[:, :, :],
                                         op0=ALU.is_lt, op1=ALU.mult).then_inc(s["wtap_step"], 1)
                dve.wait_ge(s["wtap_step"], b * 3 + 1)
                dve.tensor_reduce(wsum[:, :], wtap[:, :, :], AX.X, ALU.add).then_inc(s["wtap_step"], 1)
                dve.wait_ge(s["wtap_step"], b * 3 + 2)
                dve.reciprocal(wrec[:, :], wsum[:, :]).then_inc(s["wtap_step"], 1)
                dve.wait_ge(s["wtap_step"], b * 3 + 3)
                dve.tensor_tensor(wtap[:, :, :], wtap[:, :, :], wrec[:, :].rearrange("p (n o) -> p n o", o=1).broadcast_to([128, NC, S]),
                                  ALU.mult).then_inc(s["wtap_ready"], 1)

            def body(a, b, c):
                if a is not None:
                    dve.wait_ge(s["kf_ready"], a + 1)
                    for par in range(2):
                        dve.tensor_copy(vpad[:, par, HD * par:HD * par + HD], P[0][:, 2 * S:2 * S + HD]).then_inc(s["v_ready"], 1)
                if isinstance(a, int) and a == 2:
                    dve.wait_ge(s["wsplit"], 5)
                    dve.tensor_tensor(w_b[1][:, :, :], stage[:, :, :], w_b[0][:, :, :].bitcast(F32), ALU.subtract).then_inc(s["wsplit"], 1)
                if a is not None:
                    row_max(a, 0)
                    row_max(a, 1)
                    if c is not None:
                        router(c)
                    row_max(a, 2)
                    if c is not None:
                        router_gates(c)
                    row_max(a, 3)
                    if c is not None:
                        router_picked(c)
                    row_max(a, 4)
                    if c is not None:
                        router_sum(c)
                    if b is not None:
                        dve.wait_ge(s["wo_ps"], b + 1)
                        dve.tensor_tensor(x_all[:, b, :], x_all[:, b, :], P[3][:, :], ALU.add).then_inc(s["a_done"], 1)
                        hold(dve, "a_done", b + 1)
                        moments(b, x_all[:, b, :], stats2, mv2, "stat2", "mvr2")
                    if c is not None:
                        router_scale(c)
                    row_max(a, 5)
                    if b is not None:
                        normalize(b, qn[:, :], x_all[:, b, :], mv2, rstd2, "rstdr2", "qn_ready")
                    row_max(a, 6)
                    row_max(a, 7)
                else:
                    if c is not None:
                        dve.wait_ge(s["hT_ready"], c + 1)
                        dve.wait_ge(s["hT_hi"], c + 1)
                        dve.wait_ge(s["z_ps"], c)
                        dve.tensor_tensor(h_h[1][:, :, :], h_t[:, :, :], h_h[0][:, :, :].bitcast(F32),
                                          ALU.subtract).then_inc(s["hT_lo"], 1)
                    if b is not None:
                        dve.wait_ge(s["wo_ps"], b + 1)
                        dve.tensor_tensor(x_all[:, b, :], x_all[:, b, :], P[3][:, :], ALU.add).then_inc(s["a_done"], 1)
                        hold(dve, "a_done", b + 1)
                        moments(b, x_all[:, b, :], stats2, mv2, "stat2", "mvr2")
                    if c is not None:
                        router(c)
                    if b is not None:
                        normalize(b, qn[:, :], x_all[:, b, :], mv2, rstd2, "rstdr2", "qn_ready")
                    if c is not None:
                        router_gates(c)
                        router_picked(c)
                        router_sum(c)
                        router_scale(c)
                        dve.wait_ge(s["z_ps"], c + 1)
                        gated(dve, c, P[7])
                if b is not None:
                    dve.wait_ge(s["fq_ps"], b + 1)
                    dve.wait_ge(s["fv_ready"], b * 4 + 4)
                    dve.tensor_tensor(pr1[:, :], P[4][:, :], fv[:, :], ALU.mult)
                    dve.tensor_tensor(pr2[:, :], P[4][:, :], fvx[:, :], ALU.mult).then_inc(s["pr_ready"], 1)
                if a is not None:
                    dve.wait_ge(s["maxT_ps"], a + 1)
                    freed(dve, "rank_ready", a * 32)
                    dve.tensor_scalar(nm_hi[:, :], P[2][0:HEADS, 0:S], -1.0, None, ALU.mult).then_inc(s["nmax_ready"], 1)
                    dve.wait_ge(s["nmax_ready"], a * 2 + 1)
                    dve.scalar_tensor_tensor(out=nm_lo[:, :], in0=P[2][0:HEADS, 0:S], scalar=-1.0, in1=nm_hi[:, :],
                                             op0=ALU.mult, op1=ALU.subtract).then_inc(s["nmax_ready"], 1)
                if c is not None:
                    dve.wait_ge(s["zgT_hi"], c + 1)
                    dve.tensor_tensor(zg_h[1][:, :, :], P[6][:, :].rearrange("p (c t) -> p c t", c=NC), zg_h[0][:, :, :].bitcast(F32),
                                      ALU.subtract).then_inc(s["zgT_ready"], 1)
                if a is not None:
                    if isinstance(a, int) and a == 0:
                        dve.wait_ge(s["in_x1"], 16)
                    if isinstance(a, int) and a == 1:
                        dve.wait_ge(s["in_x"], 16)
                    moments(a + 1, x_all[:, a + 1, :], stats1, mv1, "stat1", "mvr1")
                if b is not None:
                    delays(b)
                if a is not None:
                    dve.wait_ge(s["xnT_ps"], a + 1)
                    normalize(a + 1, xn[:, :], x_all[:, a + 1, :], mv1, rstd1, "rstdr1", "xn_ready")
                if c is not None:
                    dve.wait_ge(s["ffn_ps"], c + 1)
                    dve.tensor_tensor(x_all[:, c, :], x_all[:, c, :], P[7][:, :], ALU.add).then_inc(s["c_done"], 1)
                if b is not None:
                    dve.wait_ge(s["fw_ps"], b + 1)
                    dve.tensor_tensor(pr1[:, :], P[4][:, :], fv[:, :], ALU.mult)
                    dve.tensor_tensor(pr2[:, :], P[4][:, :], fvx[:, :], ALU.mult).then_inc(s["pe_ready"], 1)
                    dve.wait_ge(s["fwo_ps"], b + 1)
                    dve.wait_ge(s["gv_ready"], b * 3 + 3)
                    dve.tensor_tensor(po1[:, :], P[5][:, :], gv[:, :], ALU.mult)
                    dve.tensor_tensor(po2[:, :], P[5][:, :], gvx[:, :], ALU.mult).then_inc(s["po_ready"], 1)
                if a is not None:
                    dve.wait_ge(s["den_ps"], a + 1)
                    freed(dve, "attn_ready", a)
                    dve.reciprocal(rsum[:, :], P[3][:, :]).then_inc(s["rsum_ready"], 1)
                if b is not None:
                    dve.wait_ge(s["inv_ps"], b + 1)
                    dve.tensor_tensor(x_all[:, b, :], x_all[:, b, :], P[4][:, :], ALU.add).then_inc(s["b_done"], 1)
                    hold(dve, "b_done", b + 1)
                    moments(b, x_all[:, b, :], stats3, mv3, "stat3", "mvr3")
                if a is not None:
                    dve.wait_ge(s["pv_ps"], a + 1)
                    dve.wait_ge(s["rsum_ready"], a + 1)
                    dve.tensor_tensor(rsum[:, :], P[2][:, :], rsum[:, :], ALU.mult).then_inc(s["attn_f"], 1)
                if b is not None:
                    freed(dve, "hT_ps", b)
                    normalize(b, hn[:, :], x_all[:, b, :], mv3, rstd3, "rstdr3", "hn_ready")
                if a is not None:
                    dve.wait_ge(s["attn_hi"], a + 1)
                    dve.tensor_tensor(attn_h[1][:, :], rsum[:, :], attn_h[0][:, :].bitcast(F32), ALU.subtract).then_inc(s["attn_ready"], 1)

            dve.wait_ge(s["in_x0"], 16)
            moments(0, x_all[:, 0, :], stats1, mv1, "stat1", "mvr1")
            normalize(0, xn[:, :], x_all[:, 0, :], mv1, rstd1, "rstdr1", "xn_ready")
            dve.wait_ge(s["const_ready"], NCONST)
            dve.wait_ge(s["in_small"], 16 * 7)
            for h in range(HEADS):
                dve.scalar_tensor_tensor(out=tab[:, h // HC, h % HC, :], in0=positions[:, :], scalar=slopes[:, h:h + 1], in1=maskt[:, :],
                                         op0=ALU.mult, op1=ALU.add).then_inc(s["tab_ready"], 1)
            turns(dve, body)

        @block.tensor
        def _(pe):
            ident = mat[:, IDENT, :]

            def transposes(bank, src, signal):
                for n in range(NC):
                    last = pe.transpose(P[bank][:, n * 128:(n + 1) * 128], src[:, n * 128:(n + 1) * 128], ident)
                last.then_inc(s[signal], 1)

            def halves(acc, lhs, rhs, start, stop):
                pe.matmul(acc, lhs[0], rhs[1], start=start, stop=False)
                pe.matmul(acc, lhs[1], rhs[0], start=False, stop=False)
                return pe.matmul(acc, lhs[0], rhs[0], start=False, stop=stop)

            def context(b, n):
                if n:
                    pe.wait_ge(s["fv_ready"], b * 4 + 4)
                else:
                    freed(pe, "po_ready", b)
                halves(P[5][:, :], [m[:, n, :] for m in mctx], [r[:, :] for r in ctx_h], True, True).then_inc(s["fctx_ps"], 1)

            def scores_by_query(a, n):
                if n == 0:
                    pe.wait_ge(s["kb_ready"], a + 1)
                    pe.wait_ge(s["qhi_ready"], a * 2 + 1)
                    pe.wait_ge(s["v_ready"], a * 2 + 2)
                if n == 1:
                    pe.wait_ge(s["q1_ready"], a * 2 + 1)
                if n == 2:
                    pe.wait_ge(s["q1_ready"], a * 2 + 2)
                if 3 <= n < 7:
                    pe.wait_ge(s["ql_max"], a * 8 + n - 2)
                ch, hf = n // 2, n % 2
                pe.matmul(P[BY_QUERY[n]][:, :], q_hi[:, ch, :], kb_hi[:, 4 * hf:4 * hf + 4, :], start=True, stop=False)
                pe.matmul(P[BY_QUERY[n]][:, :], idb[:, :], tab[:, ch, 4 * hf:4 * hf + 4, :], start=False, stop=True).then_inc(s["ql_ps"], 1)

            def scores_by_key(a, n):
                j = JORDER[n]
                if n == 0:
                    pe.wait_ge(s["kstack_ready"], a + 1)
                    pe.wait_ge(s["q_stacked"], a * 96 + 96)
                    pe.wait_ge(s["rank_ready"], a * 32 + 32)
                if n >= 3:
                    pe.wait_ge(s["exp_ready"], a * 8 + n - 2)
                pe.matmul(P[BY_KEY[n % 3]][:, :], maskt[:, :], idb[:, :].rearrange("p (o t) -> p o t", o=1).broadcast_to([128, NC, S]),
                          start=True, stop=False)
                pe.matmul(P[BY_KEY[n % 3]][:, :], k_stack[0:KROWS, :], q_stack[:, j, :, :], start=False, stop=True).then_inc(s["kl_ps"], 1)

            def body(a, b, c):
                first = isinstance(a, int) and a == 0
                if a is not None:
                    pe.wait_ge(s["xn_ready"], a + 1)
                    freed(pe, "exp_ready", a * 8)
                    transposes(0, xn[:, :], "xnT_ps")
                if isinstance(b, int) and b == 0:
                    pe.wait_ge(s["in_mat"], 16)
                    pe.wait_ge(s["mctx_ready"], 2)
                if b is not None:
                    pe.wait_ge(s["ctx_ready"], b + 1)
                    context(b, 0)
                if a is not None:
                    if first:
                        pe.wait_ge(s["in_wqkv"], 16)
                    pe.wait_ge(s["xnT_ready"], a + 1)
                    for k in range(NC):
                        last = pe.matmul(P[0][32 * k:32 * k + 32, 0:S], w_qkv[:, k, HEADS * HD:], xn_t[:, k, :], start=True, stop=True)
                    last.then_inc(s["kv4_ps"], 1)
                def h_transposes(c):
                    if c is not None:
                        if isinstance(c, int) and c == 0:
                            pe.wait_ge(s["in_wr"], 16 * (NC + 1))
                        pe.wait_ge(s["hn_ready"], c + 1)
                        freed(pe, "zgT_ready", c)
                        transposes(6, hn[:, :], "hT_ps")

                for n in range(NC):
                    if a is not None:
                        for k in range(NC):
                            last = pe.matmul(P[1 + n // 2][:, n % 2 * S:n % 2 * S + S], w_qkv[:, k, n * 128:(n + 1) * 128], xn_t[:, k, :],
                                             start=(k == 0), stop=(k == NC - 1))
                            if n == 2 and k == 1:
                                h_transposes(c)
                        if n % 2:
                            last.then_inc(s["q_ps"], 1)
                        if n == 1 and not first:
                            pe.wait_ge(s["attn_f"], a)
                        if n == 0:
                            if first:
                                pe.wait_ge(s["in_small"], 16 * 7)
                            pe.wait_ge(s["kvt_ready"], a + 1)
                            pe.matmul(P[0][:, S:2 * S], sel_k[:, :], kv_t[:, :], start=True, stop=True)
                            pe.matmul(P[0][:, 2 * S:2 * S + HD], kv_t[:, :], sel_v[:, :], start=True, stop=True).then_inc(s["kv_ps"], 1)
                    if a is None and n == 2:
                        h_transposes(c)
                def router_queries(c):
                    if c is not None:
                        freed(pe, "c_done", c)
                        pe.wait_ge(s["hT_ready"], c + 1)
                        for k in range(NC):
                            last = pe.matmul(P[7][32 * k:32 * k + 32, 0:S], w_rq[:, k, :], h_t[:, k, :], start=True, stop=True)
                        last.then_inc(s["rq_ps"], 1)

                def router_scores(c):
                    if c is not None:
                        pe.wait_ge(s["hT_hi"], c + 1)
                        pe.wait_ge(s["rq_ready"], c + 1)
                        pe.matmul(P[6][:, 128:128 + EXPERTS], rq_t[:, :], w_keys[:, :], start=True, stop=True).then_inc(s["sc_ps"], 1)

                if a is not None:
                    router_queries(c)
                if first:
                    pe.wait_ge(s["in_small"], 16 * 7)
                    pe.wait_ge(s["tab_ready"], HEADS)
                if a is not None:
                    scores_by_query(a, 0)
                    scores_by_query(a, 1)
                    router_scores(c)
                if b is not None:
                    pe.wait_ge(s["attn_ready"], b + 1)
                    if isinstance(b, int) and b == 0:
                        pe.wait_ge(s["wsplit"], 2)
                for k in range(NC):
                    if b is not None:
                        last = halves(P[3][:, :], [m[:, k * 128:(k + 1) * 128] for m in attn_h], [w[:, k, :] for w in w_o], k == 0, k == NC - 1)
                        if k == NC - 1:
                            last.then_inc(s["wo_ps"], 1)
                    if a is not None and k == 0:
                        scores_by_query(a, 2)
                        scores_by_query(a, 3)
                    if a is not None and k == 1:
                        scores_by_query(a, 4)
                if a is None:
                    router_queries(c)
                    router_scores(c)
                if c is not None:
                    pe.wait_ge(s["hT_lo"], c + 1)
                    if isinstance(c, int) and c == 0:
                        pe.wait_ge(s["wsplit"], 4)
                for k in range(NC):
                    if c is not None:
                        last = halves(P[7][:, :], [m[:, k, :] for m in h_h], [w[:, k, :] for w in w_a], k == 0, k == NC - 1)
                        if k == NC - 1:
                            last.then_inc(s["z_ps"], 1)
                    if a is not None and k in (0, 1):
                        scores_by_query(a, 5 + k)
                if a is not None:
                    if b is not None:
                        pe.wait_ge(s["a_done"], b + 1)
                    scores_by_query(a, 7)
                if b is not None:
                    pe.wait_ge(s["qn_ready"], b + 1)
                    freed(pe, "b_done", b)
                    pe.matmul(P[4][:, :], mat[:, FWD, :], qn[:, :], start=True, stop=True).then_inc(s["fq_ps"], 1)
                    context(b, 1)
                if c is not None:
                    pe.wait_ge(s["zg_ready"], c + 1)
                    transposes(6, zg[:, :], "zgT_ps")
                if a is not None:
                    pe.wait_ge(s["ql_max"], a * 8 + 8)
                    pe.transpose(P[2][0:HEADS, 0:S], rowmax[:, :, :].rearrange("p j c -> p (j c)"), ident).then_inc(s["maxT_ps"], 1)
                if b is not None:
                    pe.wait_ge(s["pr_ready"], b + 1)
                    for n in range(NC):
                        ch = slice(n * 128, (n + 1) * 128)
                        pe.matmul(P[4][:, ch], pr1[:, ch], mat[:, CR1, :], start=True, stop=False)
                        last = pe.matmul(P[4][:, ch], pr2[:, ch], mat[:, CR2, :], start=False, stop=True)
                    last.then_inc(s["corr_ps"], 1)
                if c is not None:
                    pe.wait_ge(s["zgT_ready"], c + 1)
                    if isinstance(c, int) and c == 0:
                        pe.wait_ge(s["wsplit"], 6)
                    for k in range(NC):
                        last = halves(P[7][:, :], [m[:, k, :] for m in zg_h], [w[:, k, :] for w in w_b], k == 0, k == NC - 1)
                    last.then_inc(s["ffn_ps"], 1)
                if first:
                    pe.wait_ge(s["in_rank"], 16 * 4)

                def values(half, bank, lhs):
                    pe.wait_ge(s["exp_ready"], a * 8 + 4 * half + 4)
                    for j in JORDER[4 * half:4 * half + 4]:
                        g = 32 * (j // 2)
                        last = pe.matmul(P[bank][g:g + 32, :], lhs[:, j % 2, :], probs[:, j, :], start=(half == 0), stop=(half == 1))
                    return last

                for n in range(8):
                    if a is not None:
                        scores_by_key(a, n)
                if a is not None:
                    if b is not None:
                        pe.wait_ge(s["a_done"], b + 1)
                    pe.wait_ge(s["nmax_ready"], a * 2 + 2)
                    values(0, 3, onesp)
                    values(0, 2, vpad)
                if b is not None:
                    pe.wait_ge(s["wtap_ready"], b + 1)
                    transposes(4, wtap[:, :, :].rearrange("p n t -> p (n t)"), "wT_ps")
                if a is not None:
                    values(1, 3, onesp).then_inc(s["den_ps"], 1)
                if b is not None:
                    pe.wait_ge(s["wT_ready"], b + 1)
                    pe.matmul(P[4][:, :], mat[:, FWD, :], wtap_t[:, :], start=True, stop=True).then_inc(s["fw_ps"], 1)
                    pe.wait_ge(s["gv_ready"], b * 3 + 3)
                    pe.matmul(P[5][:, :], mat[:, GWD, :], wtap_t[:, :], start=True, stop=True).then_inc(s["fwo_ps"], 1)
                if a is not None:
                    values(1, 2, vpad).then_inc(s["pv_ps"], 1)
                if b is not None:
                    pe.wait_ge(s["pe_ready"], b + 1)
                    pe.matmul(P[4][:, :], mat[:, EI1, :], pr1[:, :], start=True, stop=False)
                    pe.matmul(P[4][:, :], mat[:, EI2, :], pr2[:, :], start=False, stop=False)
                    pe.wait_ge(s["po_ready"], b + 1)
                    pe.matmul(P[4][:, :], mat[:, OI1, :], po1[:, :], start=False, stop=False)
                    pe.matmul(P[4][:, :], mat[:, OI2, :], po2[:, :], start=False, stop=True).then_inc(s["inv_ps"], 1)

            pe.wait_ge(s["in_ident"], 16)
            turns(pe, body)


def _constants():
    import numpy as np
    L, hlf = S, S // 2
    t = np.arange(L)[:, None].astype(np.float64)
    f = np.arange(hlf)[None, :].astype(np.float64)
    we, wo_ = 2 * np.pi * f / L, 2 * np.pi * (f + 0.5) / L
    fwd = np.concatenate([np.cos(we * t), -np.sin(we * t)], 1)
    fwd[:, hlf] = np.cos(np.pi * t[:, 0])
    gwd = np.concatenate([np.cos(wo_ * t), -np.sin(wo_ * t)], 1)
    gv = gwd.copy()
    gv[L - 1] -= gwd.sum(0)
    tt = t.T
    ce, se = 2 * np.cos(we.T * tt) / L, 2 * np.sin(we.T * tt) / L
    base1 = np.concatenate([ce, ce], 0)
    base1[hlf] = np.cos(np.pi * tt[0]) / L
    base1[0] = 1.0 / L
    cr1 = base1
    cr2 = np.concatenate([se, -se], 0)
    cr2[0] = 0.0
    cr2[hlf] = 0.0
    ei1 = base1
    ei2 = np.concatenate([-se, se], 0)
    ei2[0] = 1.0
    ei2[hlf] = 0.0
    co, so = 2 * np.cos(wo_.T * tt) / L, 2 * np.sin(wo_.T * tt) / L
    oi1 = np.concatenate([co, co], 0)
    oi2 = np.concatenate([-so, so], 0)
    mats = np.stack([fwd, gv, gwd, cr1, cr2, ei1 / 2, ei2 / 2, oi1 / 2, oi2 / 2, np.eye(L)], 1).astype(np.float32)
    bf = mybir.dt.np(BF16)
    slopes = ((2.0 ** (-2.0 ** (-(np.log2(HEADS) - 3)))) ** np.arange(1, HEADS + 1)).astype(np.float32)
    pos = np.arange(S)
    rank_l = np.zeros((128, 128), bf)
    rank_l[QROWS:QROWS + 3] = pos.astype(bf)
    rank_l[QROWS + 3:QROWS + 5] = 1.0
    rank_r = np.zeros((3, HC, NC, S), bf)
    rest = slopes.copy()
    for n in range(3):
        part = rest.astype(bf)
        rank_r[n] = part.reshape(NC, HC, 1).transpose(1, 0, 2)
        rest = rest - part.astype(np.float32)
    blockmask = (np.arange(128)[:, None] // HD == np.arange(HC)[None, :]).astype(np.float32)
    parts = np.zeros((128, 3), np.float32)
    for n, (_, kp) in enumerate(PAIRS):
        parts[n * HD:(n + 1) * HD, kp] = 1.0
    ones_pad = np.zeros((128, 2, 32), np.float32)
    ones_pad[:, 0, :HD] = 1.0
    ones_pad[:, 1, HD:] = 1.0
    row, col = np.arange(128)[:, None], np.arange(128)[None, :]
    sum_k = (row % 32 == col % HD).astype(np.float32)
    sum_v = (row % 32 == HD + np.arange(HD)[None, :]).astype(np.float32)
    return {"mats": mats, "pos": np.tile(pos.astype(np.float32), (128, 1)), "slope": np.tile(slopes, (128, 1)),
            "rank_l": rank_l, "rank_r": rank_r, "blockmask": blockmask, "parts": parts, "ones_pad": ones_pad,
            "identb": np.eye(128).astype(bf), "causal": np.where(pos[None, :] > pos[:, None], np.float32(-1e30), np.float32(0)).astype(bf),
            "sum_k": sum_k, "sum_v": sum_v}


def kernel(x, ctx_4096, L0_attn_Wqkv, L0_attn_Wo, L0_ffn_A_w, L0_ffn_B_w, L0_ffn_Wq_w, L0_ffn_keys):
    import numpy as np
    import concourse.bacc as bacc
    from concourse.bass_utils import run_bass_kernel_spmd

    nc = bacc.Bacc("TRN2", target_bir_lowering=False, num_devices=1)
    arrays = {
        "x": x, "ctx": ctx_4096, "wqkv": L0_attn_Wqkv, "wo": L0_attn_Wo, "a_t": np.asarray(L0_ffn_A_w).T,
        "b_t": np.asarray(L0_ffn_B_w).T, "wq_t": np.asarray(L0_ffn_Wq_w).T, "keys_t": np.asarray(L0_ffn_keys).T,
        **_constants(),
    }
    arrays = {f"in_{n}": np.ascontiguousarray(v) for n, v in arrays.items()}
    args = [nc.dram_tensor(n, v.shape, mybir.dt.from_np(v.dtype), kind="ExternalInput").ap() for n, v in arrays.items()]
    out = nc.dram_tensor("out", (NB, S, D), F32, kind="ExternalOutput").ap()
    decoder_layer(nc, *args, out)
    r = run_bass_kernel_spmd(nc, [arrays], core_ids=[0])
    return r.results[0]["out"]
```
